# Optimizing a Trainium2 kernel written in Bass

```python
import numpy as np
import jax
import jax.numpy as jnp

def _softmax(x, axis=-1):
    return jax.nn.softmax(x, axis=axis)

def _gelu(x):
    return jax.nn.gelu(x, approximate=True)

def _silu(x):
    return jax.nn.silu(x)

def _sigmoid(x):
    return jax.nn.sigmoid(x)

def _layernorm(x, axis=-1, eps=1e-05):
    m = jnp.mean(x, axis=axis, keepdims=True)
    v = jnp.var(x, axis=axis, keepdims=True)
    return (x - m) / jnp.sqrt(v + eps)

def _scatter_add(tgt, idx, src, axis=0):
    return tgt.at[idx].add(src)

def _segment_sum(src, seg, n):
    return jax.ops.segment_sum(src, seg, n)
kernel_name = 'mk_decoder_preln_d1_seqx_r4_7cb0f6'

def setup_inputs(seed: int=0):
    np.random.seed(seed)
    _w = jnp.asarray

    def _rec_inputs():
        import jax
        import jax.numpy as jnp
        _rk = jax.random.key(seed)
        x = -0.000125 + 0.9999 * jax.random.normal(jax.random.fold_in(_rk, 1), (2, 1024, 256), jnp.float32)
        _lenS = 1024 - jax.random.randint(jax.random.fold_in(_rk, 7), (2,), 0, max(1, 1024 // 4) + 1, jnp.int32)
        _lenS2 = 77 - jax.random.randint(jax.random.fold_in(_rk, 8), (2,), 0, max(1, 77 // 4) + 1, jnp.int32)
        _ctx_768P = jax.random.normal(jax.random.fold_in(_rk, 11), (2, 16, 192), jnp.float32)
        _ctx_768c = jax.random.dirichlet(jax.random.fold_in(_rk, 511), 0.3 * jnp.ones((16,), jnp.float32), (2, 77))
        _ctx_768t = jnp.einsum('bsk,bkd->bsd', _ctx_768c, _ctx_768P)
        _ctx_768t = _ctx_768t * jax.lax.rsqrt(jnp.mean(jnp.square(_ctx_768t)) + 1e-12) * 0.953939
        ctx_768 = 0.00272024 + 0.999456 * (_ctx_768t + 0.3 * jax.random.normal(jax.random.fold_in(_rk, 611), (2, 77, 192), jnp.float32))
        return (x, ctx_768)
    x, ctx_768 = _rec_inputs()

    def _L0_attn_setup():
        import jax, jax.numpy as jnp
        import numpy as np
        DIM = 256
        H = 16
        DH = DIM // H
        NF = 64
        EPS = 1e-06
        key = jax.random.key(seed)
        ks = jax.random.split(key, 10)
        B, L = (4, 1024)
        s = 1.0 / np.sqrt(DIM)
        x = jax.random.normal(ks[0], (B, L, DIM), dtype=jnp.float32)
        Wq = jax.random.normal(ks[1], (DIM, DIM), dtype=jnp.float32) * s
        Wk = jax.random.normal(ks[2], (DIM, DIM), dtype=jnp.float32) * s
        Wv = jax.random.normal(ks[3], (DIM, DIM), dtype=jnp.float32) * s
        Wo = jax.random.normal(ks[4], (DIM, DIM), dtype=jnp.float32) * s
        bq = jax.random.normal(ks[5], (DIM,), dtype=jnp.float32) * s
        bk = jax.random.normal(ks[6], (DIM,), dtype=jnp.float32) * s
        bv = jax.random.normal(ks[7], (DIM,), dtype=jnp.float32) * s
        bo = jax.random.normal(ks[8], (DIM,), dtype=jnp.float32) * s
        Wrf = jax.random.normal(ks[9], (1, H, DH, NF), dtype=jnp.float32)
        return {'x': x, 'Wq': Wq, 'bq': bq, 'Wk': Wk, 'bk': bk, 'Wv': Wv, 'bv': bv, 'Wo': Wo, 'bo': bo, 'Wrf': Wrf}
    _L0_attn_all = _L0_attn_setup()
    _L0_attn_in = {k: v for k, v in _L0_attn_all.items() if k in ('Wq', 'bq', 'Wk', 'bk', 'Wv', 'bv', 'Wo', 'bo', 'Wrf')}
    del _L0_attn_all

    def _L0_xattn_setup():
        import jax, jax.numpy as jnp
        import numpy as np
        N_HEADS = 8
        D_EMBED = 256
        D_CROSS = 192
        D_HEAD = D_EMBED // N_HEADS
        key = jax.random.key(seed)
        ks = jax.random.split(key, 10)
        B, SQ, SKV = (8, 1024, 77)
        scale_e = 1.0 / np.sqrt(D_EMBED)
        scale_c = 1.0 / np.sqrt(D_CROSS)
        return {'x': jax.random.normal(ks[0], (B, SQ, D_EMBED), dtype=jnp.float32), 'y': jax.random.normal(ks[1], (B, SKV, D_CROSS), dtype=jnp.float32), 'Wq': jax.random.normal(ks[2], (D_EMBED, D_EMBED), dtype=jnp.float32) * scale_e, 'bq': jnp.zeros((D_EMBED,), dtype=jnp.float32), 'Wk': jax.random.normal(ks[3], (D_CROSS, D_EMBED), dtype=jnp.float32) * scale_c, 'bk': jnp.zeros((D_EMBED,), dtype=jnp.float32), 'Wv': jax.random.normal(ks[4], (D_CROSS, D_EMBED), dtype=jnp.float32) * scale_c, 'bv': jnp.zeros((D_EMBED,), dtype=jnp.float32), 'Wo': jax.random.normal(ks[5], (D_EMBED, D_EMBED), dtype=jnp.float32) * scale_e, 'bo': jnp.zeros((D_EMBED,), dtype=jnp.float32)}
    _L0_xattn_all = _L0_xattn_setup()
    _L0_xattn_in = {k: v for k, v in _L0_xattn_all.items() if k in ('Wq', 'bq', 'Wk', 'bk', 'Wv', 'bv', 'Wo', 'bo')}
    del _L0_xattn_all

    def _L0_ffn_setup():
        import jax, jax.numpy as jnp
        import numpy as np
        B, N, DIM = (2, 512, 256)
        HEADS, DIM_HEAD, EXPERTS = (8, 64, 8)
        SCALE = DIM_HEAD ** (-0.5)
        key = jax.random.key(seed)
        ks = jax.random.split(key, 6)
        dim_inner = HEADS * DIM_HEAD
        return {'x': jax.random.normal(ks[0], (B, N, DIM), jnp.float32), 'w_q': jax.random.normal(ks[1], (DIM, dim_inner), jnp.float32) * 0.02, 'w_k': jax.random.normal(ks[2], (DIM, dim_inner), jnp.float32) * 0.02, 'w_gate': jax.random.normal(ks[3], (DIM, HEADS * EXPERTS), jnp.float32) * 0.02, 'value_experts': jax.random.normal(ks[4], (EXPERTS, HEADS, DIM, DIM_HEAD), jnp.float32) * 0.02, 'output_experts': jax.random.normal(ks[5], (EXPERTS, HEADS, DIM_HEAD, DIM), jnp.float32) * 0.02}
    _L0_ffn_all = _L0_ffn_setup()
    _L0_ffn_in = {k: v for k, v in _L0_ffn_all.items() if k in ('w_q', 'w_k', 'w_gate', 'value_experts', 'output_experts')}
    del _L0_ffn_all
    return {'x': x, 'ctx_768': ctx_768, 'L0_attn_Wq': _L0_attn_in['Wq'], 'L0_attn_bq': _L0_attn_in['bq'], 'L0_attn_Wk': _L0_attn_in['Wk'], 'L0_attn_bk': _L0_attn_in['bk'], 'L0_attn_Wv': _L0_attn_in['Wv'], 'L0_attn_bv': _L0_attn_in['bv'], 'L0_attn_Wo': _L0_attn_in['Wo'], 'L0_attn_bo': _L0_attn_in['bo'], 'L0_attn_Wrf': _L0_attn_in['Wrf'], 'L0_xattn_Wq': _L0_xattn_in['Wq'], 'L0_xattn_bq': _L0_xattn_in['bq'], 'L0_xattn_Wk': _L0_xattn_in['Wk'], 'L0_xattn_bk': _L0_xattn_in['bk'], 'L0_xattn_Wv': _L0_xattn_in['Wv'], 'L0_xattn_bv': _L0_xattn_in['bv'], 'L0_xattn_Wo': _L0_xattn_in['Wo'], 'L0_xattn_bo': _L0_xattn_in['bo'], 'L0_ffn_w_q': _L0_ffn_in['w_q'], 'L0_ffn_w_k': _L0_ffn_in['w_k'], 'L0_ffn_w_gate': _L0_ffn_in['w_gate'], 'L0_ffn_value_experts': _L0_ffn_in['value_experts'], 'L0_ffn_output_experts': _L0_ffn_in['output_experts']}

def reference(x, ctx_768, L0_attn_Wq, L0_attn_bq, L0_attn_Wk, L0_attn_bk, L0_attn_Wv, L0_attn_bv, L0_attn_Wo, L0_attn_bo, L0_attn_Wrf, L0_xattn_Wq, L0_xattn_bq, L0_xattn_Wk, L0_xattn_bk, L0_xattn_Wv, L0_xattn_bv, L0_xattn_Wo, L0_xattn_bo, L0_ffn_w_q, L0_ffn_w_k, L0_ffn_w_gate, L0_ffn_value_experts, L0_ffn_output_experts):
    import jax
    import jax.numpy as jnp

    def _L0_attn_ref(x, Wq, bq, Wk, bk, Wv, bv, Wo, bo, Wrf):
        import jax, jax.numpy as jnp
        import numpy as np
        DIM = 256
        H = 16
        DH = DIM // H
        NF = 64
        EPS = 1e-06
        B, L, _ = x.shape
        W0 = Wrf[0]

        def split_heads(y):
            return y.reshape(B, L, H, DH).transpose(0, 2, 1, 3)
        q = split_heads(x @ Wq.T + bq)
        k = split_heads(x @ Wk.T + bk)
        v = split_heads(x @ Wv.T + bv)
        logits = jnp.einsum('bhld,hdf->bhlf', k, W0) - 0.5 * jnp.sum(k * k, axis=-1, keepdims=True)
        alpha = jax.nn.softmax(logits.reshape(B, H, L * NF), axis=2)
        alpha = alpha.reshape(B, H, L, NF)
        N = jnp.einsum('bhlf,bhld->bhfd', alpha, v)
        D = jnp.sum(alpha, axis=2)
        phi = jax.nn.softmax(jnp.einsum('bhld,hdf->bhlf', q, W0), axis=-1)
        num = jnp.einsum('bhlf,bhfd->bhld', phi, N)
        den = jnp.einsum('bhlf,bhf->bhl', phi, D)
        out = num / (den[..., None] + EPS)
        ctx = out.transpose(0, 2, 1, 3).reshape(B, L, DIM)
        return ctx @ Wo.T + bo

    def _L0_xattn_ref(x, y, Wq, bq, Wk, bk, Wv, bv, Wo, bo):
        import jax, jax.numpy as jnp
        import numpy as np
        N_HEADS = 8
        D_EMBED = 256
        D_CROSS = 192
        D_HEAD = D_EMBED // N_HEADS
        B, SQ, _ = x.shape
        q = x @ Wq + bq
        k = y @ Wk + bk
        v = y @ Wv + bv
        q = q.reshape(B, SQ, N_HEADS, D_HEAD).transpose(0, 2, 1, 3)
        k = k.reshape(B, -1, N_HEADS, D_HEAD).transpose(0, 2, 1, 3)
        v = v.reshape(B, -1, N_HEADS, D_HEAD).transpose(0, 2, 1, 3)
        scale = 1.0 / jnp.sqrt(jnp.asarray(D_HEAD, dtype=q.dtype))
        weight = jnp.einsum('bhqd,bhkd->bhqk', q, k) * scale
        weight = jax.nn.softmax(weight, axis=-1)
        out = jnp.einsum('bhqk,bhkd->bhqd', weight, v)
        out = out.transpose(0, 2, 1, 3).reshape(B, SQ, D_EMBED)
        return out @ Wo + bo

    def _L0_ffn_ref(x, w_q, w_k, w_gate, value_experts, output_experts):
        import jax, jax.numpy as jnp
        import numpy as np
        B, N, DIM = (2, 512, 256)
        HEADS, DIM_HEAD, EXPERTS = (8, 64, 8)
        SCALE = DIM_HEAD ** (-0.5)
        b, n, _ = x.shape
        q = (x @ w_q).reshape(b, n, HEADS, DIM_HEAD).transpose(0, 2, 1, 3)
        k = (x @ w_k).reshape(b, n, HEADS, DIM_HEAD).transpose(0, 2, 1, 3)
        gates = jax.nn.sigmoid((x @ w_gate).reshape(b, n, HEADS, EXPERTS).transpose(0, 2, 1, 3))
        sel = jnp.argmax(gates, axis=-1)
        gm = jax.nn.one_hot(sel, EXPERTS, dtype=x.dtype) * gates
        values = jnp.einsum('bhne,ehdk,bnd->bhnk', gm, value_experts, x)
        sim = jnp.einsum('bhid,bhjd->bhij', q * SCALE, k)
        causal_mask = jnp.triu(jnp.ones((n, n), dtype=bool), 1)
        sim = jnp.where(causal_mask, jnp.finfo(sim.dtype).min, sim)
        attn = jax.nn.softmax(sim, axis=-1)
        out = jnp.einsum('bhij,bhjk->bhik', attn, values)
        out = jnp.einsum('bhne,ehkd,bhnk->bhnd', gm, output_experts, out)
        return out.sum(axis=1)
    x = x + _L0_attn_ref(_layernorm(x, axis=-1), L0_attn_Wq, L0_attn_bq, L0_attn_Wk, L0_attn_bk, L0_attn_Wv, L0_attn_bv, L0_attn_Wo, L0_attn_bo, L0_attn_Wrf)
    x = x + _L0_xattn_ref(_layernorm(x, axis=-1), ctx_768, L0_xattn_Wq, L0_xattn_bq, L0_xattn_Wk, L0_xattn_bk, L0_xattn_Wv, L0_xattn_bv, L0_xattn_Wo, L0_xattn_bo)
    x = x + _L0_ffn_ref(_layernorm(x, axis=-1), L0_ffn_w_q, L0_ffn_w_k, L0_ffn_w_gate, L0_ffn_value_experts, L0_ffn_output_experts)
    return x

_drawn_inputs = setup_inputs


def setup_inputs(seed=0):
    import zlib

    import numpy as np

    out = dict(_drawn_inputs(seed))
    spreads = {'L0_xattn_bq': (0.0, 0.368),
     'L0_xattn_bk': (0.0, 0.8),
     'L0_xattn_bv': (0.0, 0.1),
     'L0_xattn_bo': (0.0, 0.1)}
    factors = {'L0_ffn_w_q': 8.0,
     'L0_ffn_w_k': 8.0,
     'L0_ffn_w_gate': 5.841,
     'L0_ffn_value_experts': 5.367,
     'L0_ffn_output_experts': 5.423}
    for name, (base, spread) in spreads.items():
        noise = np.random.default_rng([zlib.crc32(name.encode()), seed]).standard_normal(out[name].shape)
        drawn = base * np.exp(spread * noise) if base else spread * noise
        out[name] = jnp.asarray(drawn.astype(out[name].dtype))
    for name, factor in factors.items():
        out[name] = (out[name] * factor).astype(out[name].dtype)
    return out
```

```python
import concourse.bass as bass
from concourse import mybir
from contextlib import ExitStack


def decoder_layer(nc: bass.Bass, d, out: bass.AP):
    fp32 = mybir.dt.float32
    fp32r = mybir.dt.float32r
    bf16 = mybir.dt.bfloat16
    u32 = mybir.dt.uint32
    ALU = mybir.AluOpType
    ACT = mybir.ActivationFunctionType
    AX = mybir.AxisListType
    ACROSS_MAX = bass.bass_isa.ReduceOp.max

    P = 128
    B, S, D = d["x"].shape
    TT = S // P
    CH = 512
    NC = S // CH
    TC = CH // P
    DA = D // P
    HALF = P // 2
    H1, HD1, NF = 16, 16, 64
    V1W = HD1 + 1
    PAIRS1 = H1 // 2
    EPS_LN = 1e-5
    H2, HD2 = 8, 32
    DCP, SKV = d["ctxT"].shape[0], d["ctxT"].shape[2] // B
    V2W = HD2 + 1
    K2 = H2 * SKV
    K2C = -(-K2 // P)
    K2L = K2 - (K2C - 1) * P
    FIRST2 = [c * P // SKV for c in range(K2C)]
    HEADS2 = [(min((c + 1) * P, K2) - 1) // SKV + 1 - FIRST2[c] for c in range(K2C)]
    WIDE2 = max(HEADS2) * V2W
    SCALE2 = float(HD2) ** -0.5
    H3, HD3, E3 = 8, 64, 8
    PAIRS3 = H3 // 2
    SCALE3 = float(HD3) ** -0.5
    HK = H3 * HD3
    G = H3 * E3
    BLOCKS = [(c, j) for c in range(NC) for j in range(TC * (c + 1))]
    NB = len(BLOCKS)
    NEP = E3 * PAIRS3
    SLOTS = 3

    ctx = ExitStack()
    with ctx:
        def sb(name, shape, dt=fp32):
            return ctx.enter_context(nc.sbuf_tensor(name, shape, dt))

        X = sb("X", [P, B, TT, D])
        WkT, WqT, WvT, WoT = (sb(n, [P, DA, D]) for n in ("WkT", "WqT", "WvT", "WoT"))
        W0 = sb("W0", [P, DA, H1 // DA * NF])
        W2q, W2o = sb("W2q", [P, DA, D]), sb("W2o", [P, DA, D])
        Wg = sb("Wg", [P, DA, G])
        W3q, W3k = sb("W3q", [P, DA, HK]), sb("W3k", [P, DA, HK])
        experts = sb("experts", [P, SLOTS, 4 * D])
        cols = sb("cols", [P, 8])
        rows = sb("rows", [P, 4, D])
        const = sb("const", [P, 4 * P + 8 + G + E3])
        ident = const[:, 0:P]
        eps_blk = const[:, P:2 * P]
        neg_f = const[:, 2 * P:4 * P].rearrange("p (i s) -> p i s", i=2)
        head_of = const[:, 4 * P:4 * P + 8]
        pick_f = const[:, 4 * P + 8:4 * P + 8 + G]
        iota_e = const[:, 4 * P + 8 + G:]
        neg_delta = sb("neg_delta", [TT, TT, P])
        ident_b = sb("ident_b", [P, P], bf16)
        neg = sb("neg", [P, 2, P], bf16)
        kblk = sb("kblk", [P, B, DA, 4 * SKV])
        vblk = sb("vblk", [P, B, K2C, WIDE2])
        xT = sb("xT", [P, DA, S])
        xn = sb("xn", [P, 2, D])
        st = sb("st", [P, 2, 6])
        mv = sb("mv", [P, 2, 2])
        ve = sb("ve", [P, 2, 1])
        minus_half = sb("minus_half", [P, 1])
        rstd = sb("rstd", [P, 2, 1])
        cx = sb("cx", [P, 2, D])
        cxT = sb("cxT", [P, 2, DA, P])
        top = sb("top", [P, 2, H1])
        rc = sb("rc", [P, 2, H1])
        N1 = sb("N1", [P, PAIRS1, 2 * V1W])

        REGION = 20 * 1024
        region = sb("region", [P, REGION])
        at = [0]

        def view(words):
            v = region[:, at[0]:at[0] + words]
            at[0] += words
            assert at[0] <= REGION, at
            return v

        W2k = view(2 * D)[0:DCP].rearrange("p (i n) -> p i n", i=2)
        W2v = view(2 * D)[0:DCP].rearrange("p (i n) -> p i n", i=2)
        ctxT = view(2 * B * SKV)[0:DCP].rearrange("p (i n) -> p i n", i=2)
        v2 = view(B * H2 * V2W)[0:SKV].rearrange("p (b h w) -> p b h w", b=B, h=H2)
        at[0] = 0
        E1 = view(TT * H1 * NF).rearrange("p (t n) -> p t n", t=TT)
        qT = view(DA * S).rearrange("p (a s) -> p a s", a=DA)
        kT = view(DA * S).rearrange("p (a s) -> p a s", a=DA)
        phi_all = view(2 * H1 * NF)
        phi = phi_all.rearrange("p (i n) -> p i n", i=2)
        kk = phi_all.rearrange("p (a s) -> p a s", a=DA)
        phT = view(2 * H1 * NF).rearrange("p (i n) -> p i n", i=2)
        V1 = view(TT * H1 * V1W).rearrange("p (t h w) -> p t h w", t=TT, h=H1)
        mk_all = view(TT * H1)
        mk = mk_all.rearrange("p (t h) -> p t h", t=TT)
        ak_all = view(TT * H1)
        ak = ak_all.rearrange("p (t h) -> p t h", t=TT)
        ak_top = view(H1)
        k_max = view(H1)

        at[0] = 0
        V3 = view(TT * PAIRS3 * 3 * HD3).rearrange("p (t a k) -> p t a k", t=TT, a=PAIRS3)
        V3_heads = V3.rearrange("p t a (i k) -> p t a i k", i=3)[:, :, :, 0:3:2, :]
        V3_ones = V3[:, :, :, HD3:2 * HD3]
        oT = view(PAIRS3 * S).rearrange("p (a s) -> p a s", a=PAIRS3)
        shared = at[0]
        PT = view(NB * CH).rearrange("p (n s) -> p n s", n=NB)
        after = at[0]
        at[0] = shared
        g3, gw, one = (view(TT * G).rearrange("p (t h e) -> p t h e", t=TT, h=H3) for _ in range(3))
        gidx = view(TT * H3).rearrange("p (t h) -> p t h", t=TT)
        at[0] = shared
        mo = view(2 * S).rearrange("p (i s) -> p i s", i=2)
        at[0] = after
        raw = view(2 * S).rearrange("p (i s) -> p i s", i=2)
        hot = view(TT * G).rearrange("p (t h e) -> p t h e", t=TT, h=H3)
        gtop = view(TT * H3).rearrange("p (t h) -> p t h", t=TT)
        mx = view(2 * TT).rearrange("p (i n) -> p i n", i=2)
        rden = view(CH)
        kst, kx, qq, qx = ([sb(f"{n}{i}", [P, S], fp32r) for i in range(2)]
                           for n in ("kst", "kx", "qq", "qx"))
        picks = lambda e: (kst[0], kst[1], qq[0], qq[1])[e // 2][:, e % 2 * HK:(e % 2 + 1) * HK]
        gT = sb("gT", [P, S], fp32r)

        ps = ctx.enter_context(nc.psum_tensor("ps", [P, 8, CH], fp32))

        PER = dict(
            var_ready=3 * TT, rstd_ready=3 * TT, xn_ready=3 * TT, xnT_ps=3 * TT, xT_ready=3 * TT, bias_added=2 * TT,
            proj_ps=4 * NC, proj_sb=4 * NC, v_ps=TT, v_sb=TT, kk_sb=1, kk_ps=1,
            fk_ps=TT, fk_sub=TT, e_ready=TT, ak_top_ready=1, k_max_ready=1, ak_ready=1, w_ready=1, wv_ready=1,
            n_ps=1, n_blk=1, za_ps=1, n_ready=1,
            f_ps=2 * TT, f_sub=2 * TT, f_exp=2 * TT, fT_ps=2 * TT, fT_a=2 * TT, fT_v=2 * TT,
            num_ps=2 * TT, cx_ready=2 * TT, cxT_ps=2 * TT, cxT_sb=2 * TT, y_ps=2 * TT,
            q2_ps=2 * NC, q2_sb=2 * NC,
            gate_ps=1, gate_exp=1, g_ready=1, gT_ps=1, gT_a=1, gT_v=1,
            val_ps=TT * E3, val_a=TT, val_v=TT * (E3 - 1), v3_ready=TT + 1, picks_ready=E3,
            qk_ps=PAIRS3 * 2 * NC, qk_sb=PAIRS3 * 2 * NC, qq_ready=2 * H3, kst_qx_ready=3 * H3, kx_ready=H3,
            s_ps=H3 * TT, s_max=H3 * TT, mxT_ps=H3, m_row=H3,
            st_ps=H3 * NB, pt_ready=H3 * NB, av_used=H3 * NB, av_sb=H3 * NC,
            mask_ps=NEP, mo_ready=NEP, mo_used=NEP, out_ready=TC,
        )
        sem = {n: ctx.enter_context(nc.semaphore(n)) for n in PER}
        single = ("x_first", "x_second", "x_next", "w_a", "w_b", "w_c", "v2_placed", "stored",
                  "cleared", "casts", "c2k_ps", "c2v_ps", "c2k_sb", "c2v_sb", "dve_step")
        x_first, x_second, x_next, w_a, w_b, w_c, v2_placed, stored, \
            cleared, casts, c2k_ps, c2v_ps, c2k_sb, c2v_sb, dve_step = (
                ctx.enter_context(nc.semaphore(n)) for n in single)
        expert_in = [ctx.enter_context(nc.semaphore(f"expert_in{i}")) for i in range(SLOTS)]
        block = ctx.enter_context(nc.Block())

        def until(eng, name, b, k):
            if b * PER[name] + k > 0:
                eng.wait_ge(sem[name], b * PER[name] + k)

        SETUP = 10
        LOADS_A, LOADS_B, LOADS_C = 8, 7, 4
        PIECES = 2 * E3
        V2_RUNS = [(h, max(h * SKV, c * P), min((h + 1) * SKV, (c + 1) * P), c)
                   for c in range(K2C) for h in range(FIRST2[c], FIRST2[c] + HEADS2[c])]

        @block.sync
        def _(sp):
            xv = d["x"].rearrange("b (t p) e -> b p t e", p=P)
            ov = out.rearrange("b (t p) e -> b p t e", p=P)
            sp.dma_start(X[:, 0, 0:TC, :], xv[0, :, 0:TC, :]).then_inc(x_first, 16)
            sp.dma_start(const[:, :], d["const"]).then_inc(w_a, 16)
            sp.dma_start(X[:, 0, TC:TT, :], xv[0, :, TC:TT, :]).then_inc(x_second, 16)
            sp.dma_start(rows[:, :, :], d["rows"]).then_inc(w_a, 16)
            sp.dma_start(cols[:, :], d["cols"]).then_inc(w_a, 16)
            for w, n in ((WkT, "WkT"), (WqT, "WqT"), (WvT, "WvT"), (W0, "W0")):
                sp.dma_start(w[:, :, :], d[n]).then_inc(w_a, 16)
            sp.dma_start(neg_delta[:, :, :], d["neg_delta"]).then_inc(w_a, 16)
            for w, n in ((W2k, "W2k"), (W2v, "W2v"), (ctxT, "ctxT")):
                sp.dma_start(w, d[n]).then_inc(w_b, 16)
            for w, n in ((WoT, "WoT"), (W2q, "W2q"), (W2o, "W2o"), (Wg, "Wg")):
                sp.dma_start(w[:, :, :], d[n]).then_inc(w_b, 16)
            sp.dma_start(W3q[:, :, :], d["W3q"]).then_inc(w_c, 16)
            sp.dma_start(W3k[:, :, :], d["W3k"]).then_inc(w_c, 16)
            sp.dma_start(X[:, 1, :, :], xv[1]).then_inc(x_next, 16)
            sp.wait_ge(cleared, 2)
            sp.wait_ge(c2v_sb, B)
            for bb in range(B):
                for h, r0, r1, c in V2_RUNS:
                    w0 = (h - FIRST2[c]) * V2W
                    sp.dma_start(vblk[r0 - c * P:r1 - c * P, bb, c, w0:w0 + V2W],
                                 v2[r0 - h * SKV:r1 - h * SKV, bb, h, :]).then_inc(v2_placed, 16)

            def piece_used(b, q):
                if q < E3:
                    until(sp, "val_ps", b, (q + 1) * TT)
                else:
                    until(sp, "mo_used", b, (q - E3 + 1) * PAIRS3)

            for b in range(B):
                for q in range(PIECES):
                    g = b * PIECES + q
                    if g >= SLOTS:
                        piece_used((g - SLOTS) // PIECES, (g - SLOTS) % PIECES)
                    sp.dma_start(experts[:, g % SLOTS, :],
                                 d["value_experts" if q < E3 else "output_experts"][:, q % E3, :]
                                 ).then_inc(expert_in[g % SLOTS], 16)
                for i in range(TC):
                    until(sp, "out_ready", b, i + 1)
                    sp.dma_start(ov[b, :, 2 * i:2 * i + 2, :], X[:, b, 2 * i:2 * i + 2, :]).then_inc(stored, 16)
            sp.wait_ge(stored, B * TC * 16)

        @block.gpsimd
        def _(pool):
            setup = [(minus_half[:, :], -0.5), (vblk[:, :, :, :], 0.0), (kblk[:, :, :, :], 0.0), (N1[:, :, :], 0.0)]
            for i in range(2):
                oth = HALF * (1 - i)
                setup += [(qx[i][oth:oth + HALF, :].bitcast(fp32), 0.0), (kx[i][oth:oth + HALF, :].bitcast(fp32), 0.0),
                          (kx[i][oth:oth + TT, :].bitcast(fp32), 1.0)]
            for n, (what, value) in enumerate(setup):
                pool.memset(what, value).then_inc(cleared, 1)
                pool.wait_ge(cleared, n + 1)
            for b in range(B):
                for a in range(3):
                    for s in range(TT + 1):
                        if s < TT:
                            until(pool, "var_ready", b, a * TT + s + 1)
                            pool.tensor_tensor(rstd[:, s % 2, :], ve[:, s % 2, :], minus_half[:, :],
                                               ALU.pow).then_inc(sem["rstd_ready"], 1)
                            until(pool, "rstd_ready", b, a * TT + s + 1)
                        if s and a < 2:
                            t = s - 1
                            until(pool, "xn_ready", b, a * TT + t + 1)
                            if b + a + t == 0:
                                pool.wait_ge(w_a, 16 * LOADS_A)
                            pool.tensor_tensor(X[:, b, t, :], X[:, b, t, :], rows[:, 1 + 2 * a, :],
                                               ALU.add).then_inc(sem["bias_added"], 1)
                            until(pool, "bias_added", b, a * TT + t + 1)
                    if a == 0:
                        until(pool, "ak_top_ready", b, 1)
                        pool.partition_all_reduce(k_max, ak_top, P, ACROSS_MAX).then_inc(sem["k_max_ready"], 1)
                until(pool, "val_v", b, TT * (E3 - 1))
                pool.memset(V3_ones, 1.0).then_inc(sem["v3_ready"], 1)
                for t in range(TT):
                    until(pool, "v3_ready", b, t + 1)
                    pool.tensor_tensor(V3_heads[:, t], V3_heads[:, t],
                                       gtop[:, t, :].rearrange("p (a i) -> p a i", i=2).unsqueeze(3)
                                       .broadcast_to([P, PAIRS3, 2, HD3]), ALU.mult).then_inc(sem["v3_ready"], 1)
                until(pool, "v3_ready", b, TT + 1)
                for h in range(H3):
                    own = HALF * (h % 2)
                    until(pool, "kx_ready", b, h)
                    until(pool, "qk_sb", b, (h // 2 + 1) * 2 * NC)
                    if h >= 2:
                        until(pool, "st_ps", b, (h - 1) * NB)
                    pool.tensor_copy(kx[h % 2][own:own + HALF, :], raw[own:own + HALF, 1, :]
                                     ).then_inc(sem["kx_ready"], 1)
                for e in range(E3):
                    until(pool, "st_ps", b, (H3 - 1 + e // 2 % 2) * NB)
                    until(pool, "kx_ready", b, H3)
                    until(pool, "picks_ready", b, e)
                    pool.tensor_copy(picks(e).rearrange("p (h k) -> p h k", h=H3),
                                     pick_f.rearrange("p (h e) -> p h e", h=H3)[:, :, e:e + 1]
                                     .broadcast_to([P, H3, HD3])).then_inc(sem["picks_ready"], 1)

        @block.scalar
        def _(act):
            def copy(dst, src, name):
                act.activation(dst, src, ACT.Copy).then_inc(sem[name], 1)

            def norm_evac(b, a, t):
                until(act, "xnT_ps", b, a * TT + t + 1)
                copy(xT[:, :, t * P:(t + 1) * P], ps[:, 7, 0:D].rearrange("p (a s) -> p a s", a=DA), "xT_ready")

            for b in range(B):
                for t in range(TT):
                    norm_evac(b, 0, t)
                if b == 0:
                    act.wait_ge(w_a, 16 * LOADS_A)
                    act.wait_ge(cleared, 3)
                    for bb in range(B):
                        act.wait_ge(c2k_ps, bb + 1)
                        for a in range(DA):
                            for h in range(4):
                                r = HD2 * h
                                last = act.activation(kblk[r:r + HD2, bb, a, h * SKV:(h + 1) * SKV],
                                                      ps[r:r + HD2, a, 0:SKV], ACT.Identity,
                                                      bias=cols[r:r + HD2, 6 + a:7 + a])
                        last.then_inc(c2k_sb, 1)
                for n in range(4 * NC):
                    which, a, c = n // (2 * NC), n // NC % 2, n % NC
                    bias = 2 * (1 - which) + a
                    until(act, "proj_ps", b, n + 1)
                    act.activation((kT, qT)[which][:, a, c * CH:(c + 1) * CH], ps[:, 2 + n % 2, :], ACT.Identity,
                                   bias=cols[:, bias:bias + 1]).then_inc(sem["proj_sb"], 1)
                    if n == 2 * NC - 1:
                        until(act, "proj_sb", b, 2 * NC)
                        act.activation(kk, kT, ACT.Square).then_inc(sem["kk_sb"], 1)
                for t in range(TT):
                    until(act, "fk_sub", b, t + 1)
                    act.activation(E1[:, t, :], E1[:, t, :], ACT.Exp).then_inc(sem["e_ready"], 1)
                until(act, "ak_ready", b, 1)
                act.activation(ak_all, ak_all, ACT.Exp).then_inc(sem["w_ready"], 1)

                for a in range(2):
                    if a == 1:
                        for n in range(2 * NC):
                            c, half = n // 2, n % 2
                            until(act, "q2_ps", b, n + 1)
                            act.activation(qT[:, half, c * CH:(c + 1) * CH], ps[:, 2 + n % 2, :], ACT.Identity,
                                           bias=cols[:, 4 + half:5 + half]).then_inc(sem["q2_sb"], 1)
                    wide, scale = (H1 * NF, 1.0) if a == 0 else (K2, SCALE2)
                    for s in range(TT + 7):
                        if s < TT:
                            until(act, "f_sub", b, a * TT + s + 1)
                            act.activation(phi[:, s % 2, 0:wide], phi[:, s % 2, 0:wide], ACT.Exp,
                                           scale=scale).then_inc(sem["f_exp"], 1)
                        if 0 <= (t := s - 1) < TT:
                            until(act, "fT_ps", b, a * TT + t + 1)
                            if t >= 2:
                                until(act, "num_ps", b, a * TT + t - 1)
                            copy(phT[:, t % 2, 0:CH], ps[:, 0, :], "fT_a")
                        if 0 <= (t := s - 3) < TT:
                            until(act, "cxT_ps", b, a * TT + t + 1)
                            if t >= 2:
                                until(act, "y_ps", b, a * TT + t - 1)
                            copy(cxT[:, t % 2, :, :], ps[:, 4, 0:D].rearrange("p (a s) -> p a s", a=DA), "cxT_sb")
                        if 0 <= (t := s - 6) < TT:
                            norm_evac(b, a + 1, t)
                until(act, "gate_ps", b, 1)
                act.activation(g3.rearrange("p t h e -> p (t h e)"), ps[:, 6, :], ACT.Exp,
                               scale=-1.0).then_inc(sem["gate_exp"], 1)
                for t in range(TT):
                    until(act, "val_ps", b, t + 1)
                    copy(V3_heads[:, t], ps[:, t % 4, :].rearrange("p (a i k) -> p a i k", i=2, k=HD3), "val_a")
                until(act, "gT_ps", b, 1)
                copy(gT[0:G, :].rearrange("p (i s) -> p i s", i=NC), ps[0:G, 4:4 + NC, :], "gT_a")

                def qk_evac(p):
                    for n in range(2 * NC):
                        i, c = n // NC, n % NC
                        until(act, "qk_ps", b, p * 2 * NC + n + 1)
                        if p and n == 0:
                            until(act, "kst_qx_ready", b, 6 * p)
                            until(act, "kx_ready", b, 2 * p)
                        act.activation(raw[:, i, c * CH:(c + 1) * CH], ps[:, 6, :], ACT.Copy,
                                       scale=(SCALE3, 1.0)[i]).then_inc(sem["qk_sb"], 1)

                def split(h):
                    i, own, oth = h % 2, HALF * (h % 2), HALF * (1 - h % 2)
                    until(act, "qk_sb", b, (h // 2 + 1) * 2 * NC)
                    if h >= 2:
                        until(act, "st_ps", b, (h - 1) * NB)
                    copy(qq[i][own:own + HALF, :], raw[own:own + HALF, 0, :], "qq_ready")
                    copy(qq[i][oth:oth + HALF, :], raw[own:own + HALF, 0, :], "qq_ready")

                qk_evac(0)
                split(0)
                for h in range(H3):
                    if h + 1 < H3:
                        if h % 2:
                            qk_evac(h // 2 + 1)
                        split(h + 1)
                    for n, (c, j) in enumerate(BLOCKS):
                        lo = max(0, j - TC * c) * P
                        until(act, "st_ps", b, h * NB + n + 1)
                        if h:
                            until(act, "av_used", b, (h - 1) * NB + n + 1)
                        act.activation(PT[:, n, lo:CH], ps[:, 4 + n % 2, 0:CH - lo], ACT.Exp
                                       ).then_inc(sem["pt_ready"], 1)

        @block.vector
        def _(dve):
            steps = [0]

            def step(ins):
                steps[0] += 1
                ins.then_inc(dve_step, 1)
                dve.wait_ge(dve_step, steps[0])

            def norm_stats(b, a, t):
                i = t % 2
                step(dve.bn_stats(st[:, i, :], X[:, b, t, :]))
                step(dve.bn_aggr(mv[:, i, :], st[:, i, :]))
                dve.tensor_scalar(ve[:, i, :], mv[:, i, 1:2], EPS_LN, None, ALU.add).then_inc(sem["var_ready"], 1)

            def norm_apply(b, a, t):
                i, idx = t % 2, a * TT + t
                x = X[:, b, t, :]
                until(dve, "rstd_ready", b, idx + 1)
                if idx >= 2:
                    until(dve, "xnT_ps", b, idx - 1)
                dve.tensor_scalar(xn[:, i, :], x, mv[:, i, 0:1], rstd[:, i, 0:1],
                                  ALU.subtract, ALU.mult).then_inc(sem["xn_ready"], 1)

            dve.wait_ge(x_first, 16)
            for b in range(B):
                for t in range(TT):
                    if b == 0 and t == TC:
                        dve.wait_ge(x_second, 16)
                    if b == 1 and t == 0:
                        dve.wait_ge(x_next, 16)
                    norm_stats(b, 0, t)
                    if t:
                        norm_apply(b, 0, t - 1)
                norm_apply(b, 0, TT - 1)
                if b == 0:
                    dve.wait_ge(w_a, 16 * LOADS_A)
                    dve.tensor_copy(ident_b[:, :], ident).then_inc(casts, 1)
                    dve.tensor_copy(neg[:, :, :], neg_f).then_inc(casts, 1)
                    step(dve.memset(v2[:, :, :, HD2:V2W], 1.0))
                    for bb in range(B):
                        dve.wait_ge(c2v_ps, bb + 1)
                        dve.tensor_tensor(v2[:, bb, :, 0:HD2],
                                          ps[0:SKV, 4, 0:D].rearrange("p (h k) -> p h k", h=H2),
                                          rows[0:SKV, 2, :].rearrange("p (h k) -> p h k", h=H2),
                                          ALU.add).then_inc(c2v_sb, 1)
                step(dve.memset(V1[:, :, :, HD1:V1W], 1.0))
                for t in range(TT):
                    until(dve, "v_ps", b, t + 1)
                    dve.tensor_tensor(V1[:, t, :, 0:HD1],
                                      ps[:, 4 + t % 2, 0:D].rearrange("p (h k) -> p h k", h=H1),
                                      rows[:, 0, :].rearrange("p (h k) -> p h k", h=H1),
                                      ALU.add).then_inc(sem["v_sb"], 1)
                for t in range(TT):
                    f = ps[:, 2 - 2 * (t % 2):4 - 2 * (t % 2), :].rearrange("p a (h f) -> p (a h) f", f=NF)
                    until(dve, "fk_ps", b, t + 1)
                    step(dve.tensor_reduce(mk[:, t, :], f, AX.X, ALU.max))
                    if b == 0 and t == 0:
                        dve.wait_ge(v2_placed, 16 * B * len(V2_RUNS))
                    dve.tensor_tensor(E1[:, t, :].rearrange("p (h f) -> p h f", f=NF), f,
                                      mk[:, t, :].unsqueeze(2).broadcast_to([P, H1, NF]),
                                      ALU.subtract).then_inc(sem["fk_sub"], 1)
                until(dve, "kk_ps", b, 1)
                step(dve.scalar_tensor_tensor(ak_all, ps[:, 6, 0:TT * H1], -0.5, mk_all, ALU.mult, ALU.add))
                dve.tensor_reduce(ak_top, ak.rearrange("p t h -> p h t"), AX.X, ALU.max
                                  ).then_inc(sem["ak_top_ready"], 1)
                until(dve, "k_max_ready", b, 1)
                dve.tensor_tensor(ak, ak, k_max.unsqueeze(1).broadcast_to([P, TT, H1]),
                                  ALU.subtract).then_inc(sem["ak_ready"], 1)
                until(dve, "w_ready", b, 1)
                dve.tensor_tensor(V1.rearrange("p t h w -> p (t h) w"), V1.rearrange("p t h w -> p (t h) w"),
                                  ak_all.unsqueeze(2).broadcast_to([P, TT * H1, V1W]),
                                  ALU.mult).then_inc(sem["wv_ready"], 1)
                until(dve, "n_ps", b, 1)
                n1 = ps[:, 7, 0:PAIRS1 * 2 * V1W].rearrange("p (a w) -> p a w", a=PAIRS1)
                if b == 0:
                    dve.wait_ge(cleared, 4)
                dve.tensor_copy(N1[0:HALF, :, 0:V1W], n1[0:HALF, :, 0:V1W]).then_inc(dve_step, 1)
                steps[0] += 1
                dve.tensor_copy(N1[HALF:P, :, V1W:2 * V1W], n1[HALF:P, :, V1W:2 * V1W]).then_inc(sem["n_blk"], 1)
                until(dve, "za_ps", b, 1)
                den = N1[:, :, :].rearrange("p a (i w) -> p (a i) w", i=2)[:, :, HD1]
                dve.tensor_tensor(den, den, ps[:, 6, 0:2 * PAIRS1], ALU.add).then_inc(sem["n_ready"], 1)

                for a in range(2):
                    H, HD, W = (H1, HD1, V1W) if a == 0 else (H2, HD2, V2W)
                    for s in range(TT + 6):
                        if s < TT:
                            t, i = s, s % 2
                            until(dve, "f_ps", b, a * TT + t + 1)
                            if a == 0:
                                f = ps[:, 2:4, :].rearrange("p a (h f) -> p (a h) f", f=NF)
                                o = phi[:, i, :].rearrange("p (h f) -> p h f", f=NF)
                                m, mb = top[:, i, 0:H], top[:, i, 0:H].unsqueeze(2).broadcast_to([P, H, NF])
                            else:
                                f = ps[:, 2:4, 0:4 * SKV].rearrange("p a (h f) -> p a h f", f=SKV)
                                o = phi[:, i, 0:K2].rearrange("p (a h f) -> p a h f", a=DA, f=SKV)
                                m = top[:, i, 0:H].rearrange("p (a h) -> p a h", a=DA)
                                mb = m.unsqueeze(3).broadcast_to([P, DA, 4, SKV])
                            step(dve.tensor_reduce(m, f, AX.X, ALU.max))
                            if t >= 2:
                                until(dve, "fT_ps", b, a * TT + t - 1)
                            dve.tensor_tensor(o, f, mb, ALU.subtract).then_inc(sem["f_sub"], 1)
                        if 0 <= (t := s - 1) < TT:
                            until(dve, "fT_ps", b, a * TT + t + 1)
                            if t >= 2:
                                until(dve, "num_ps", b, a * TT + t - 1)
                            if a == 0:
                                dve.tensor_copy(phT[:, t % 2, CH:2 * CH], ps[:, 1, :]).then_inc(sem["fT_v"], 1)
                            else:
                                dve.tensor_copy(phT[0:K2L, t % 2, CH:CH + P], ps[0:K2L, 1, 0:P]
                                                ).then_inc(sem["fT_v"], 1)
                        if 0 <= (t := s - 2) < TT:
                            i = t % 2
                            num = ps[:, 6, 0:H * W].rearrange("p (h w) -> p h w", w=W)
                            until(dve, "num_ps", b, a * TT + t + 1)
                            step(dve.reciprocal(rc[:, i, 0:H], num[:, :, HD]))
                            if t >= 2:
                                until(dve, "cxT_ps", b, a * TT + t - 1)
                            dve.tensor_tensor(cx[:, i, :].rearrange("p (h k) -> p h k", h=H), num[:, :, 0:HD],
                                              rc[:, i, 0:H].unsqueeze(2).broadcast_to([P, H, HD]),
                                              ALU.mult).then_inc(sem["cx_ready"], 1)
                        if 0 <= (t := s - 5) < TT:
                            norm_apply(b, a + 1, t)
                        if 0 <= (t := s - 4) < TT:
                            until(dve, "y_ps", b, a * TT + t + 1)
                            until(dve, "bias_added", b, a * TT + t + 1)
                            step(dve.tensor_tensor(X[:, b, t, :], ps[:, 5, 0:D], X[:, b, t, :], ALU.add))
                            norm_stats(b, a + 1, t)
                g3f, gwf, onef = (v.rearrange("p t h e -> p (t h e)") for v in (g3, gw, one))
                g3h, gwh, oneh, hoth = (v.rearrange("p t h e -> p (t h) e") for v in (g3, gw, one, hot))
                gt, gi = gtop.rearrange("p t h -> p (t h)"), gidx.rearrange("p t h -> p (t h)")
                wide = lambda v: v.unsqueeze(2).broadcast_to([P, TT * H3, E3])
                until(dve, "gate_exp", b, 1)
                step(dve.tensor_scalar(g3f, g3f, 1.0, None, ALU.add))
                step(dve.reciprocal(g3f, g3f))
                step(dve.tensor_reduce(gt, g3h, AX.X, ALU.max))
                step(dve.tensor_tensor(oneh, g3h, wide(gt), ALU.is_equal))
                step(dve.scalar_tensor_tensor(gwh, oneh, -float(E3),
                                              iota_e.unsqueeze(1).broadcast_to([P, TT * H3, E3]),
                                              ALU.mult, ALU.add))
                step(dve.tensor_reduce(gi, gwh, AX.X, ALU.min))
                step(dve.tensor_tensor(hoth, gwh, wide(gi), ALU.is_equal))
                dve.tensor_tensor(gwh, hoth, wide(gt), ALU.mult).then_inc(sem["g_ready"], 1)
                until(dve, "gT_a", b, 1)
                dve.tensor_tensor(gT[G:2 * G, :].rearrange("p (i s) -> p i s", i=NC), ps[0:G, 4:4 + NC, :],
                                  gT[0:G, :].bitcast(fp32).rearrange("p (i s) -> p i s", i=NC),
                                  ALU.subtract).then_inc(sem["gT_v"], 1)
                for n in range(TT, TT * E3):
                    e, t = n // TT, n % TT
                    until(dve, "val_ps", b, n + 1)
                    if e == 1:
                        until(dve, "val_a", b, t + 1)
                    chosen = hot[:, t, :, e].bitcast(u32).rearrange("p (a i) -> p a i", i=2)
                    dve.copy_predicated(V3_heads[:, t], chosen.unsqueeze(3).broadcast_to([P, PAIRS3, 2, HD3]),
                                        ps[:, n % 4, :].rearrange("p (a i k) -> p a i k", i=2, k=HD3)
                                        ).then_inc(sem["val_v"], 1)

                def split(h):
                    i, own, oth = h % 2, HALF * (h % 2), HALF * (1 - h % 2)
                    until(dve, "qk_sb", b, (h // 2 + 1) * 2 * NC)
                    if h >= 2:
                        until(dve, "st_ps", b, (h - 1) * NB)
                    dve.tensor_copy(kst[i][own:own + HALF, :], raw[own:own + HALF, 1, :]
                                    ).then_inc(sem["kst_qx_ready"], 1)
                    until(dve, "qq_ready", b, 2 * h + 1)
                    dve.tensor_tensor(qx[i][own:own + HALF, :], raw[own:own + HALF, 0, :],
                                      qq[i][own:own + HALF, :].bitcast(fp32), ALU.subtract
                                      ).then_inc(sem["kst_qx_ready"], 1)
                    until(dve, "kst_qx_ready", b, 3 * h + 1)
                    dve.tensor_tensor(kst[i][oth:oth + HALF, :], raw[own:own + HALF, 1, :],
                                      kst[i][own:own + HALF, :].bitcast(fp32), ALU.subtract
                                      ).then_inc(sem["kst_qx_ready"], 1)

                def maxima(h):
                    i, oth = h % 2, HALF * (1 - h % 2)
                    for t in range(TT):
                        w, bank = (t + 1) * P, 2 * (t % 2)
                        until(dve, "s_ps", b, h * TT + t + 1)
                        src = (ps[:, bank, 0:w] if w <= CH else
                               ps[:, bank:bank + 2, :].rearrange("p a s -> p (a s)")[:, 0:w])
                        if h >= 2 and t == 0:
                            until(dve, "mxT_ps", b, h - 1)
                        dve.tensor_reduce(mx[:, i, t:t + 1], src, AX.X, ALU.max).then_inc(sem["s_max"], 1)
                    until(dve, "mxT_ps", b, h + 1)
                    if b == 0 and h < 2:
                        dve.wait_ge(cleared, SETUP)
                    dve.tensor_tensor(qx[i][oth:oth + TT, :].rearrange("p (t s) -> p t s", t=TT),
                                      ps[0:TT, 6, 0:P].unsqueeze(1).broadcast_to([TT, TT, P]),
                                      neg_delta[:, :, :], ALU.mult).then_inc(sem["m_row"], 1)

                split(0)
                maxima(0)
                for h in range(H3):
                    if h + 1 < H3:
                        split(h + 1)
                        maxima(h + 1)
                    for c in range(NC):
                        own, oth = HALF * (h % 2), HALF * (1 - h % 2)
                        until(dve, "av_used", b, h * NB + sum(TC * (k + 1) for k in range(c + 1)))
                        step(dve.reciprocal(rden[own:own + HALF, :], ps[oth:oth + HALF, 7, :]))
                        dve.tensor_tensor(oT[own:own + HALF, h // 2, c * CH:(c + 1) * CH],
                                          ps[own:own + HALF, 7, :], rden[own:own + HALF, :], ALU.mult).then_inc(sem["av_sb"], 1)
                until(dve, "av_sb", b, H3 * NC)
                for n in range(NEP):
                    e, p = n // PAIRS3, n % PAIRS3
                    until(dve, "mask_ps", b, n + 1)
                    if n >= 2:
                        until(dve, "mo_used", b, n - 1)
                    bank = 2 * (n % 2)
                    dve.tensor_tensor(mo[:, n % 2, :], ps[:, bank:bank + 2, :].rearrange("p a s -> p (a s)"),
                                      oT[:, p, :], ALU.mult).then_inc(sem["mo_ready"], 1)
                until(dve, "mo_used", b, NEP)
                for i in range(TC):
                    dve.tensor_tensor(X[:, b, 2 * i:2 * i + 2, :],
                                      ps[:, 4 + i, :].rearrange("p (t n) -> p t n", t=2),
                                      X[:, b, 2 * i:2 * i + 2, :], ALU.add).then_inc(sem["out_ready"], 1)

        @block.tensor
        def _(pe):
            mm = pe.matmul

            def norm_transpose(b, a, t):
                idx = a * TT + t
                until(pe, "xn_ready", b, idx + 1)
                until(pe, "xT_ready", b, idx)
                for h in range(DA):
                    last = pe.transpose(ps[:, 7, h * P:(h + 1) * P], xn[:, t % 2, h * P:(h + 1) * P], ident)
                last.then_inc(sem["xnT_ps"], 1)

            pe.wait_ge(w_a, 16 * LOADS_A)
            for b in range(B):
                if b:
                    until(pe, "out_ready", b - 1, TC)
                for t in range(TT):
                    norm_transpose(b, 0, t)
                if b == 0:
                    pe.wait_ge(w_b, 16 * LOADS_B)
                    for bb in range(B):
                        if bb:
                            pe.wait_ge(c2k_sb, bb)
                            pe.wait_ge(c2v_sb, bb)
                        for a in range(DA):
                            for i in range(2):
                                last = mm(ps[:, a, 0:SKV], W2k[:, i, a * P:(a + 1) * P],
                                          ctxT[:, i, bb * SKV:(bb + 1) * SKV], start=(i == 0), stop=(i == 1))
                        last.then_inc(c2k_ps, 1)
                        for i in range(2):
                            last = mm(ps[0:SKV, 4, 0:D], ctxT[:, i, bb * SKV:(bb + 1) * SKV], W2v[:, i, :],
                                      start=(i == 0), stop=(i == 1))
                        last.then_inc(c2v_ps, 1)
                    pe.wait_ge(c2v_sb, B)
                    pe.wait_ge(c2k_sb, B)
                until(pe, "xT_ready", b, TT)
                for n in range(4 * NC):
                    which, a, c = n // (2 * NC), n // NC % 2, n % NC
                    if n >= 2:
                        until(pe, "proj_sb", b, n - 1)
                    for i in range(DA):
                        last = mm(ps[:, 2 + n % 2, :], (WkT, WqT)[which][:, i, a * P:(a + 1) * P],
                                  xT[:, i, c * CH:(c + 1) * CH], start=(i == 0), stop=(i == DA - 1))
                    last.then_inc(sem["proj_ps"], 1)
                for t in range(TT):
                    if t >= 2:
                        until(pe, "v_sb", b, t - 1)
                    for i in range(DA):
                        last = mm(ps[:, 4 + t % 2, 0:D], xT[:, i, t * P:(t + 1) * P], WvT[:, i, :],
                                  start=(i == 0), stop=(i == DA - 1))
                    last.then_inc(sem["v_ps"], 1)
                until(pe, "kk_sb", b, 1)
                for t in range(TT):
                    for a in range(DA):
                        c0 = t * H1 + a * 8
                        last = mm(ps[:, 6, c0:c0 + 8], kk[:, a, t * P:(t + 1) * P], head_of, start=True, stop=True)
                last.then_inc(sem["kk_ps"], 1)
                until(pe, "proj_sb", b, 4 * NC)
                for t in range(TT):
                    if t >= 2:
                        until(pe, "fk_sub", b, t - 1)
                    for a in range(DA):
                        last = mm(ps[:, 2 - 2 * (t % 2) + a, :], kT[:, a, t * P:(t + 1) * P], W0[:, a, :],
                                  start=True, stop=True)
                    last.then_inc(sem["fk_ps"], 1)
                until(pe, "e_ready", b, TT)
                until(pe, "wv_ready", b, 1)
                for p in range(PAIRS1):
                    for t in range(TT):
                        last = mm(ps[:, 7, p * 2 * V1W:(p + 1) * 2 * V1W], E1[:, t, p * P:(p + 1) * P],
                                  V1[:, t, 2 * p:2 * p + 2, :].rearrange("p h w -> p (h w)"),
                                  start=(t == 0), stop=(t == TT - 1))
                last.then_inc(sem["n_ps"], 1)
                until(pe, "n_blk", b, 1)
                mm(ps[:, 6, 0:2 * PAIRS1], eps_blk,
                   N1[:, :, :].rearrange("p a (i w) -> p (a i) w", i=2)[:, :, HD1],
                   start=True, stop=True).then_inc(sem["za_ps"], 1)
                until(pe, "n_ready", b, 1)

                for a in range(2):
                    if a == 1:
                        for n in range(2 * NC):
                            c, half = n // 2, n % 2
                            until(pe, "xT_ready", b, TT + (c + 1) * TC)
                            if n >= 2:
                                until(pe, "q2_sb", b, n - 1)
                            for i in range(DA):
                                last = mm(ps[:, 2 + n % 2, :], W2q[:, i, half * P:(half + 1) * P],
                                          xT[:, i, c * CH:(c + 1) * CH], start=(i == 0), stop=(i == DA - 1))
                            last.then_inc(sem["q2_ps"], 1)
                        until(pe, "q2_sb", b, 2 * NC)
                        pe.wait_ge(v2_placed, 16 * B * len(V2_RUNS))
                    chunks, wide = (PAIRS1, H1 * NF) if a == 0 else (K2C, K2)
                    for s in range(TT + 7):
                        if s < TT:
                            if s or a == 0:
                                until(pe, "f_sub", b, a * TT + s)
                            for i in range(DA):
                                if a == 0:
                                    last = mm(ps[:, 2 + i, :], qT[:, i, s * P:(s + 1) * P], W0[:, i, :],
                                              start=True, stop=True)
                                else:
                                    last = mm(ps[:, 2 + i, 0:4 * SKV], qT[:, i, s * P:(s + 1) * P],
                                              kblk[:, b, i, :], start=True, stop=True)
                            last.then_inc(sem["f_ps"], 1)
                        if 0 <= (t := s - 1) < TT:
                            until(pe, "f_exp", b, a * TT + t + 1)
                            until(pe, "fT_a", b, a * TT + t)
                            until(pe, "fT_v", b, a * TT + t)
                            for k in range(chunks):
                                r = min(P, wide - k * P)
                                last = pe.transpose(ps[0:r, k // TC, k % TC * P:(k % TC + 1) * P],
                                                    phi[:, t % 2, k * P:k * P + r], ident)
                            last.then_inc(sem["fT_ps"], 1)
                        if 0 <= (t := s - 2) < TT:
                            until(pe, "fT_a", b, a * TT + t + 1)
                            until(pe, "fT_v", b, a * TT + t + 1)
                            until(pe, "cx_ready", b, a * TT + t)
                            for k in range(chunks):
                                if a == 0:
                                    last = mm(ps[:, 6, k * 2 * V1W:(k + 1) * 2 * V1W],
                                              phT[:, t % 2, k * P:(k + 1) * P], N1[:, k, :],
                                              start=True, stop=True)
                                else:
                                    r = min(P, wide - k * P)
                                    w0, w = FIRST2[k] * V2W, HEADS2[k] * V2W
                                    last = mm(ps[:, 6, w0:w0 + w], phT[0:r, t % 2, k * P:(k + 1) * P],
                                              vblk[0:r, b, k, 0:w], start=(k == 0), stop=(k == chunks - 1),
                                              skip_group_check=True)
                            last.then_inc(sem["num_ps"], 1)
                        if 0 <= (t := s - 3) < TT:
                            until(pe, "cx_ready", b, a * TT + t + 1)
                            until(pe, "cxT_sb", b, a * TT + t)
                            for h in range(DA):
                                last = pe.transpose(ps[:, 4, h * P:(h + 1) * P], cx[:, t % 2, h * P:(h + 1) * P],
                                                    ident)
                            last.then_inc(sem["cxT_ps"], 1)
                        if 0 <= (t := s - 4) < TT:
                            until(pe, "cxT_sb", b, a * TT + t + 1)
                            if t >= 1:
                                until(pe, "var_ready", b, (a + 1) * TT + t)
                            for i in range(DA):
                                last = mm(ps[:, 5, 0:D], cxT[:, t % 2, i, :], (WoT, W2o)[a][:, i, :],
                                          start=(i == 0), stop=(i == DA - 1))
                            last.then_inc(sem["y_ps"], 1)
                        if 0 <= (t := s - 6) < TT:
                            norm_transpose(b, a + 1, t)

                until(pe, "xT_ready", b, 3 * TT)
                for t in range(TT):
                    for i in range(DA):
                        last = mm(ps[:, 6, t * G:(t + 1) * G], xT[:, i, t * P:(t + 1) * P], Wg[:, i, :],
                                  start=(i == 0), stop=(i == DA - 1))
                last.then_inc(sem["gate_ps"], 1)
                for n in range(TT * E3):
                    e, t = n // TT, n % TT
                    g = b * PIECES + e
                    if t == 0:
                        pe.wait_ge(expert_in[g % SLOTS], 16 * (g // SLOTS + 1))
                    if 4 <= n < 4 + TT:
                        until(pe, "val_a", b, n - 3)
                    elif n >= 4 + TT:
                        until(pe, "val_v", b, n - 3 - TT)
                    for i in range(DA):
                        last = mm(ps[:, n % 4, :], xT[:, i, t * P:(t + 1) * P],
                                  experts[:, g % SLOTS, i * HK:(i + 1) * HK], start=(i == 0), stop=(i == DA - 1))
                    last.then_inc(sem["val_ps"], 1)
                    if n == TT - 1:
                        until(pe, "g_ready", b, 1)
                        for k in range(TT):
                            last = pe.transpose(ps[0:G, 4 + k // TC, k % TC * P:(k % TC + 1) * P],
                                                gw[:, k, :, :].rearrange("p h e -> p (h e)"), ident)
                        last.then_inc(sem["gT_ps"], 1)

                def project(p):
                    for n in range(2 * NC):
                        w, c = (W3q, W3k)[n // NC], n % NC
                        until(pe, "qk_sb", b, p * 2 * NC + n)
                        if n == 0 and p:
                            until(pe, "m_row", b, 2 * p)
                        for i in range(DA):
                            last = mm(ps[:, 6, :], w[:, i, p * P:(p + 1) * P], xT[:, i, c * CH:(c + 1) * CH],
                                      start=(i == 0), stop=(i == DA - 1))
                        last.then_inc(sem["qk_ps"], 1)

                def scores(h):
                    i = h % 2
                    until(pe, "qq_ready", b, 2 * h + 2)
                    until(pe, "kst_qx_ready", b, 3 * h + 3)
                    for t in range(TT):
                        bank = 2 * (t % 2)
                        until(pe, "s_max", b, h * TT + t - 1)
                        for c in range(t // TC + 1):
                            w = min(CH, (t + 1) * P - c * CH)
                            diag = c == t // TC
                            mm(ps[:, bank + c, 0:w], qq[i][:, t * P:(t + 1) * P], kst[i][:, c * CH:c * CH + w],
                               start=True, stop=not diag)
                        last = mm(ps[:, bank + c, w - P:w], ident_b[:, :], neg[:, 0, :], start=False, stop=True)
                        last.then_inc(sem["s_ps"], 1)
                    until(pe, "s_max", b, (h + 1) * TT)
                    pe.transpose(ps[0:TT, 6, 0:P], mx[:, i, :], ident).then_inc(sem["mxT_ps"], 1)

                def weigh(h, n):
                    c, j = BLOCKS[n]
                    lo = max(0, j - TC * c) * P
                    until(pe, "pt_ready", b, h * NB + n + 1)
                    if j == 0:
                        until(pe, "av_sb", b, h * NC + c)
                    mm(ps[:, 7, lo:CH], V3[:, j, h // 2, h % 2 * HD3:(h % 2 + 2) * HD3], PT[:, n, lo:CH], start=(j == 0),
                       stop=(j == TC * (c + 1) - 1)).then_inc(sem["av_used"], 1)

                if b == 0:
                    pe.wait_ge(w_c, 16 * 2)
                    pe.wait_ge(casts, 2)
                    pe.wait_ge(cleared, SETUP)
                project(0)
                until(pe, "val_v", b, TT * (E3 - 1))
                scores(0)
                until(pe, "v3_ready", b, TT + 1)
                until(pe, "gT_v", b, 1)
                LAG = 2
                for h in range(H3):
                    i = h % 2
                    if h + 1 < H3:
                        if h % 2:
                            project(h // 2 + 1)
                        scores(h + 1)
                    until(pe, "kx_ready", b, h + 1)
                    until(pe, "m_row", b, h + 1)
                    for n, (c, j) in enumerate(BLOCKS):
                        lo = max(0, j - TC * c) * P
                        w = CH - lo
                        until(pe, "pt_ready", b, h * NB + n - 1)
                        tgt, key, query = ps[:, 4 + n % 2, :], slice(j * P, (j + 1) * P), slice(c * CH + lo, (c + 1) * CH)
                        mm(tgt[:, 0:w], kst[i][:, key], qq[i][:, query], start=True, stop=False)
                        last = mm(tgt[:, 0:w], kx[i][:, key], qx[i][:, query], start=False, stop=j < TC * c)
                        if j >= TC * c:
                            last = mm(tgt[:, 0:P], ident_b[:, :], neg[:, 1, :], start=False, stop=True)
                        last.then_inc(sem["st_ps"], 1)
                        if n >= LAG:
                            weigh(h, n - LAG)
                    for n in range(NB - LAG, NB):
                        weigh(h, n)

                def mask(n):
                    e, p = n // PAIRS3, n % PAIRS3
                    until(pe, "mo_ready", b, n - 1)
                    until(pe, "picks_ready", b, e + 1)
                    for c in range(NC):
                        last = mm(ps[:, 2 * (n % 2) + c, :], picks(e)[:, p * P:(p + 1) * P], gT[:, c * CH:(c + 1) * CH],
                                  start=True, stop=True)
                    last.then_inc(sem["mask_ps"], 1)

                mask(0)
                until(pe, "av_sb", b, H3 * NC)
                for n in range(NEP):
                    e, p = n // PAIRS3, n % PAIRS3
                    g = b * PIECES + E3 + e
                    if n + 1 < NEP:
                        mask(n + 1)
                    if p == 0:
                        pe.wait_ge(expert_in[g % SLOTS], 16 * (g // SLOTS + 1))
                    until(pe, "mo_ready", b, n + 1)
                    for t in range(TT):
                        last = mm(ps[:, 4 + t // 2, t % 2 * D:(t % 2 + 1) * D], mo[:, n % 2, t * P:(t + 1) * P],
                                  experts[:, g % SLOTS, p * D:(p + 1) * D], start=(n == 0 and t % 2 == 0),
                                  stop=(n == NEP - 1), skip_group_check=True)
                    last.then_inc(sem["mo_used"], 1)


def kernel(x, ctx_768, L0_attn_Wq, L0_attn_bq, L0_attn_Wk, L0_attn_bk, L0_attn_Wv, L0_attn_bv, L0_attn_Wo,
           L0_attn_bo, L0_attn_Wrf, L0_xattn_Wq, L0_xattn_bq, L0_xattn_Wk, L0_xattn_bk, L0_xattn_Wv,
           L0_xattn_bv, L0_xattn_Wo, L0_xattn_bo, L0_ffn_w_q, L0_ffn_w_k, L0_ffn_w_gate,
           L0_ffn_value_experts, L0_ffn_output_experts):
    import numpy as np
    import concourse.bacc as bacc
    from concourse.bass_utils import run_bass_kernel_spmd

    P = 128
    arr = lambda a: np.asarray(a)

    def halves(w):
        w = arr(w)
        return w.reshape(w.shape[0] // P, P, -1).transpose(1, 0, 2)

    x, c = arr(x), arr(ctx_768)
    B, S, D = x.shape
    DC = c.shape[2]
    f = x.dtype
    wrf = arr(L0_attn_Wrf)[0]
    H1, HD1, NF = wrf.shape
    w0 = np.zeros((2, 8, HD1, 8, NF), f)
    for h in range(H1):
        w0[h // 8, h % 8, :, h % 8, :] = wrf[h]
    ve, oe = arr(L0_ffn_value_experts), arr(L0_ffn_output_experts)
    E, H, _, K = ve.shape
    ve = ve.reshape(E, H, 2, P, K).transpose(3, 0, 2, 1, 4).reshape(P, E, 2 * H * K)
    oe = oe.reshape(E, H // 2, 2, K, D).transpose(2, 3, 0, 1, 4).reshape(P, E, H // 2 * D)
    two = lambda v: arr(v).reshape(2, P).T
    r, k = np.arange(P)[:, None], np.arange(P)[None, :]
    tri = np.where(k > r, -1e30, 0.0)
    TT = S // P
    const = np.concatenate([
        np.eye(P), np.where(r // NF == k // NF, 1e-6, 0.0), tri, tri.T,
        (r // HD1 == np.arange(8)[None, :]), (r % (H * E) == np.arange(H * E)[None, :]),
        np.tile(np.arange(E)[None, :], (P, 1))], axis=1).astype(f)
    neg_delta = np.zeros((TT, TT, P), f)
    for t in range(TT):
        neg_delta[t, t] = -1.0
    data = {
        "x": x,
        "ctxT": c.reshape(B * c.shape[1], 2, DC // 2).transpose(2, 1, 0),
        "WkT": halves(arr(L0_attn_Wk).T), "WqT": halves(arr(L0_attn_Wq).T),
        "WvT": halves(arr(L0_attn_Wv).T), "WoT": halves(arr(L0_attn_Wo).T),
        "W0": w0.reshape(2, P, 8 * NF).transpose(1, 0, 2),
        "W2q": halves(L0_xattn_Wq), "W2o": halves(L0_xattn_Wo),
        "W2k": arr(L0_xattn_Wk).reshape(2, DC // 2, D).transpose(1, 0, 2),
        "W2v": arr(L0_xattn_Wv).reshape(2, DC // 2, D).transpose(1, 0, 2),
        "Wg": halves(L0_ffn_w_gate), "W3q": halves(L0_ffn_w_q), "W3k": halves(L0_ffn_w_k),
        "value_experts": ve, "output_experts": oe,
        "cols": np.concatenate([two(L0_attn_bq), two(L0_attn_bk), two(L0_xattn_bq), two(L0_xattn_bk)], axis=1),
        "rows": np.broadcast_to(np.stack([arr(L0_attn_bv), arr(L0_attn_bo), arr(L0_xattn_bv),
                                          arr(L0_xattn_bo)])[None], (P, 4, D)),
        "const": const, "neg_delta": neg_delta,
    }
    nc = bacc.Bacc("TRN2", target_bir_lowering=False, num_devices=1)
    arrays, d = {}, {}
    from concourse import mybir
    for name, a in data.items():
        a = np.ascontiguousarray(a)
        arrays[f"in_{name}"] = a
        d[name] = nc.dram_tensor(f"in_{name}", a.shape, mybir.dt.from_np(a.dtype), kind="ExternalInput").ap()
    out = nc.dram_tensor("out_0", (B, S, D), mybir.dt.from_np(x.dtype), kind="ExternalOutput").ap()
    decoder_layer(nc, d, out)
    got = run_bass_kernel_spmd(nc, [arrays], core_ids=[0])
    return got.results[0]["out_0"]
```

```python
import concourse.bass as bass
from concourse import mybir
from contextlib import ExitStack


def decoder_layer(nc: bass.Bass, d, out: bass.AP):
    fp32 = mybir.dt.float32
    fp32r = mybir.dt.float32r
    bf16 = mybir.dt.bfloat16
    u32 = mybir.dt.uint32
    ALU = mybir.AluOpType
    ACT = mybir.ActivationFunctionType
    AX = mybir.AxisListType
    ACROSS_MAX = bass.bass_isa.ReduceOp.max

    P = 128
    B, S, D = d["x"].shape
    TT = S // P
    CH = 512
    NC = S // CH
    TC = CH // P
    DA = D // P
    HALF = P // 2
    H1, HD1, NF = 16, 16, 64
    V1W = HD1 + 1
    PAIRS1 = H1 // 2
    WIN = 3 * 2 * V1W
    EPS_LN = 1e-5
    H2, HD2 = 8, 32
    DCP, SKV = d["ctxT"].shape[0], d["ctxT"].shape[2] // B
    V2W = HD2 + 1
    K2 = H2 * SKV
    K2C = -(-K2 // P)
    K2L = K2 - (K2C - 1) * P
    FIRST2 = [c * P // SKV for c in range(K2C)]
    HEADS2 = [(min((c + 1) * P, K2) - 1) // SKV + 1 - FIRST2[c] for c in range(K2C)]
    WIDE2 = max(HEADS2) * V2W
    SCALE2 = float(HD2) ** -0.5
    H3, HD3, E3 = 8, 64, 8
    PAIRS3 = H3 // 2
    SCALE3 = float(HD3) ** -0.5
    HK = H3 * HD3
    G = H3 * E3
    BLOCKS = [(c, j) for c in range(NC) for j in range(TC * (c + 1))]
    NB = len(BLOCKS)
    NEP = E3 * PAIRS3
    RING = 8
    LAG = 2
    SLOTS = 3

    ctx = ExitStack()
    with ctx:
        def sb(name, shape, dt=fp32):
            return ctx.enter_context(nc.sbuf_tensor(name, shape, dt))

        X = sb("X", [P, B, TT, D])
        WkT, WqT, WvT, WoT = (sb(n, [P, DA, D]) for n in ("WkT", "WqT", "WvT", "WoT"))
        W0 = sb("W0", [P, DA, H1 // DA * NF])
        W2q, W2o = sb("W2q", [P, DA, D]), sb("W2o", [P, DA, D])
        Wg = sb("Wg", [P, DA, 96])
        W3q, W3k = sb("W3q", [P, DA, HK]), sb("W3k", [P, DA, HK])
        experts = sb("experts", [P, SLOTS, 4 * D])
        cols = sb("cols", [P, 8])
        rows = sb("rows", [P, 4, D])
        const = sb("const", [P, 4 * P + 96 + G + E3])
        ident = const[:, 0:P]
        eps_blk = const[:, P:2 * P]
        neg_f = const[:, 2 * P:4 * P].rearrange("p (i s) -> p i s", i=2)
        head_of = const[:, 4 * P:4 * P + 96]
        pick_f = const[:, 4 * P + 96:4 * P + 96 + G]
        iota_e = const[:, 4 * P + 96 + G:]
        neg_delta = sb("neg_delta", [TT, TT, P])
        ident_b = sb("ident_b", [P, P], bf16)
        neg = sb("neg", [P, 2, P], bf16)
        kblk = sb("kblk", [P, B, DA, 4 * SKV])
        vblk = sb("vblk", [P, B, K2C, WIDE2])
        xT = sb("xT", [P, DA, S])
        xn = sb("xn", [P, 2, D])
        st = sb("st", [P, 2, 6])
        mv = sb("mv", [P, 2, 2])
        ve = sb("ve", [P, 2, 1])
        minus_half = sb("minus_half", [P, 1])
        rstd = sb("rstd", [P, 2, 1])
        cx = sb("cx", [P, 2, D])
        cxT = sb("cxT", [P, 2, DA, P])
        top = sb("top", [P, 2, H1])
        rc = sb("rc", [P, 2, H1])
        N1w = sb("N1w", [P, PAIRS1, WIN])
        N1_at = lambda k: min(max(0, k - 1), PAIRS1 - 3) * 2 * V1W

        REGION = 18 * 1024
        region = sb("region", [P, REGION])
        at = [0]

        def view(words):
            v = region[:, at[0]:at[0] + words]
            at[0] += words
            assert at[0] <= REGION, at
            return v

        W2k = view(2 * D)[0:DCP].rearrange("p (i n) -> p i n", i=2)
        W2v = view(2 * D)[0:DCP].rearrange("p (i n) -> p i n", i=2)
        ctxT = view(2 * B * SKV)[0:DCP].rearrange("p (i n) -> p i n", i=2)
        v2 = view(B * H2 * V2W)[0:SKV].rearrange("p (b h w) -> p b h w", b=B, h=H2)
        at[0] = 0
        E1 = view(TT * H1 * NF).rearrange("p (t n) -> p t n", t=TT)
        kqT = view(DA * S).rearrange("p (a s) -> p a s", a=DA)
        phi_all = view(2 * H1 * NF)
        phi = phi_all.rearrange("p (i n) -> p i n", i=2)
        kk = phi_all.rearrange("p (a s) -> p a s", a=DA)
        phT = view(2 * H1 * NF).rearrange("p (i n) -> p i n", i=2)
        V1_all = view((TT - 1) * H1 * V1W + (PAIRS1 - 1) * 2 * V1W + WIN)
        V1 = V1_all[:, 0:TT * H1 * V1W].rearrange("p (t h w) -> p t h w", t=TT, h=H1)
        mk_all = view(TT * H1)
        mk = mk_all.rearrange("p (t h) -> p t h", t=TT)
        ak_all = view(TT * H1)
        ak = ak_all.rearrange("p (t h) -> p t h", t=TT)
        ak_top = view(H1)
        k_max = view(H1)

        at[0] = 0
        V3 = view(TT * PAIRS3 * 3 * HD3).rearrange("p (t a k) -> p t a k", t=TT, a=PAIRS3)
        V3_heads = V3.rearrange("p t a (i k) -> p t a i k", i=3)[:, :, :, 0:3:2, :]
        V3_ones = V3[:, :, :, HD3:2 * HD3]
        oT = view(PAIRS3 * S).rearrange("p (a s) -> p a s", a=PAIRS3)
        shared = at[0]
        PT = view(RING * CH).rearrange("p (n s) -> p n s", n=RING)
        after = at[0]
        at[0] = shared
        g3, gw, one = (view(TT * G).rearrange("p (t h e) -> p t h e", t=TT, h=H3) for _ in range(3))
        gidx = view(TT * H3).rearrange("p (t h) -> p t h", t=TT)
        at[0] = shared
        MO = 4
        mo = view(MO * CH).rearrange("p (i s) -> p i s", i=MO)
        at[0] = after
        raw = view(2 * S).rearrange("p (i s) -> p i s", i=2)
        hot = view(TT * G).rearrange("p (t h e) -> p t h e", t=TT, h=H3)
        gtop = view(TT * H3).rearrange("p (t h) -> p t h", t=TT)
        mx = view(2 * NB).rearrange("p (i n) -> p i n", i=2)
        rden = view(S)
        kst, kx, qq, qx = ([sb(f"{n}{i}", [P, S], fp32r) for i in range(2)]
                           for n in ("kst", "kx", "qq", "qx"))
        picks = lambda e: (kst[0], kst[1], qq[0], qq[1])[e // 2][:, e % 2 * HK:(e % 2 + 1) * HK]
        gT = sb("gT", [P, S], fp32r)

        ps = ctx.enter_context(nc.psum_tensor("ps", [P, 8, CH], fp32))

        PER = dict(
            var_ready=3 * TT, rstd_ready=3 * TT, xn_ready=3 * TT, xnT_ps=3 * TT, xT_ready=3 * TT, bias_added=2 * TT,
            k_ps=2 * NC, k_sb=2 * NC, q_ps=2 * NC, q_sb=2 * NC, v_ps=TT, v_sb=TT, kk_sb=1, kk_ps=1,
            fk_ps=TT, fk_sub=TT, e_ready=TT, ak_top_ready=1, k_max_ready=1, ak_ready=1, w_ready=1, wv_ready=1,
            n_ps=1, n_blk=2 * PAIRS1, za_ps=1, n_ready=3,
            f_ps=2 * TT, f_sub=2 * TT, f_exp=2 * TT, fT_ps=2 * TT, fT_sb=2 * TT,
            num_ps=2 * TT, cx_ready=2 * TT, cxT_ps=2 * TT, cxT_sb=2 * TT, y_ps=2 * TT,
            q2_ps=2 * NC, q2_sb=2 * NC,
            gate_ps=1, gate_exp=1, g_ready=1, gT_ps=1, gT_a=1, gT_v=1,
            val_ps=TT * E3, val_a=TT, val_v=TT * (E3 - 1), v3_ready=TT + 1, picks_ready=E3,
            qk_ps=PAIRS3 * 2 * NC, qk_sb=PAIRS3 * 2 * NC, qq_ready=2 * H3, kst_qx_ready=3 * H3, kx_ready=H3, o_sb=2 * H3 * NC,
            s_ps=H3 * NB, s_max=H3 * NB, tile_max=H3, mxT_ps=H3, m_row=H3,
            st_ps=H3 * NB, pt_ready=H3 * NB, av_used=H3 * NB, oT_ready=PAIRS3 * NC,
            mask_ps=NC * NEP, mo_ready=NC * NEP, mo_used=NC * NEP, out_ready=TC,
        )
        sem = {n: ctx.enter_context(nc.semaphore(n)) for n in PER}
        single = ("x_first", "x_second", "x_next", "w_a", "w_b", "w_c", "v2_placed", "stored",
                  "cleared", "casts", "c2k_ps", "c2v_ps", "c2k_sb", "c2v_sb", "dve_step")
        x_first, x_second, x_next, w_a, w_b, w_c, v2_placed, stored, \
            cleared, casts, c2k_ps, c2v_ps, c2k_sb, c2v_sb, dve_step = (
                ctx.enter_context(nc.semaphore(n)) for n in single)
        expert_in = [ctx.enter_context(nc.semaphore(f"expert_in{i}")) for i in range(SLOTS)]
        block = ctx.enter_context(nc.Block())

        def until(eng, name, b, k):
            if b * PER[name] + k > 0:
                eng.wait_ge(sem[name], b * PER[name] + k)

        SETUP = 10
        LOADS_A, LOADS_B, LOADS_C = 8, 7, 4
        N1_RUNS = [(0, 1, 0), (1, PAIRS1 - 1, 2 * V1W), (PAIRS1 - 1, PAIRS1, 4 * V1W)]
        PIECES = 2 * E3
        V2_RUNS = [(h, max(h * SKV, c * P), min((h + 1) * SKV, (c + 1) * P), c)
                   for c in range(K2C) for h in range(FIRST2[c], FIRST2[c] + HEADS2[c])]

        OFFSET = (0, 11)
        VALUES_AT = OFFSET[1] + TT + 2
        LAST = VALUES_AT + TT
        SCORES = [(t, c) for t in range(TT) for c in range(t // TC + 1)]
        SCORES_AT = {3: (0, 1, 2), 4: (3, 4), 5: (5, 6), 6: (7, 8), 7: (9, 10), 8: (11,)}
        MAX_ROW_AT = 10
        PROJECT_AT = (3, 5, 7, 9)
        MAX_BANKS, SUM_BANK = 3, (3, 7)
        ENDS = [sum(TC * (k + 1) for k in range(c + 1)) for c in range(NC)]

        def due(s, lag):
            return [(a, s - OFFSET[a] - lag) for a in range(2) if 0 <= s - OFFSET[a] - lag < TT]

        @block.sync
        def _(sp):
            xv = d["x"].rearrange("b (t p) e -> b p t e", p=P)
            ov = out.rearrange("b (t p) e -> b p t e", p=P)
            sp.dma_start(X[:, 0, 0:TC, :], xv[0, :, 0:TC, :]).then_inc(x_first, 16)
            sp.dma_start(const[:, :], d["const"]).then_inc(w_a, 16)
            sp.dma_start(X[:, 0, TC:TT, :], xv[0, :, TC:TT, :]).then_inc(x_second, 16)
            sp.dma_start(rows[:, :, :], d["rows"]).then_inc(w_a, 16)
            sp.dma_start(cols[:, :], d["cols"]).then_inc(w_a, 16)
            for w, n in ((WkT, "WkT"), (WqT, "WqT"), (WvT, "WvT"), (W0, "W0")):
                sp.dma_start(w[:, :, :], d[n]).then_inc(w_a, 16)
            sp.dma_start(neg_delta[:, :, :], d["neg_delta"]).then_inc(w_a, 16)
            for w, n in ((W2k, "W2k"), (W2v, "W2v"), (ctxT, "ctxT")):
                sp.dma_start(w, d[n]).then_inc(w_b, 16)
            for w, n in ((WoT, "WoT"), (W2q, "W2q"), (W2o, "W2o"), (Wg, "Wg")):
                sp.dma_start(w[:, :, :], d[n]).then_inc(w_b, 16)
            sp.dma_start(W3q[:, :, :], d["W3q"]).then_inc(w_c, 16)
            sp.dma_start(W3k[:, :, :], d["W3k"]).then_inc(w_c, 16)
            sp.dma_start(X[:, 1, :, :], xv[1]).then_inc(x_next, 16)
            sp.wait_ge(cleared, 2)
            sp.wait_ge(c2v_sb, B)
            for bb in range(B):
                for h, r0, r1, c in V2_RUNS:
                    w0 = (h - FIRST2[c]) * V2W
                    sp.dma_start(vblk[r0 - c * P:r1 - c * P, bb, c, w0:w0 + V2W],
                                 v2[r0 - h * SKV:r1 - h * SKV, bb, h, :]).then_inc(v2_placed, 16)

            def piece_used(b, q):
                if q < E3:
                    until(sp, "val_ps", b, (q + 1) * TT)
                else:
                    until(sp, "mo_used", b, (q - E3 + 1) * PAIRS3 * NC)

            for b in range(B):
                for q in range(PIECES):
                    g = b * PIECES + q
                    if g >= SLOTS:
                        piece_used((g - SLOTS) // PIECES, (g - SLOTS) % PIECES)
                    sp.dma_start(experts[:, g % SLOTS, :],
                                 d["value_experts" if q < E3 else "output_experts"][:, q % E3, :]
                                 ).then_inc(expert_in[g % SLOTS], 16)
                for i in range(TC):
                    until(sp, "out_ready", b, i + 1)
                    sp.dma_start(ov[b, :, 2 * i:2 * i + 2, :], X[:, b, 2 * i:2 * i + 2, :]).then_inc(stored, 16)
            sp.wait_ge(stored, B * TC * 16)

        @block.gpsimd
        def _(pool):
            setup = [(minus_half[:, :], -0.5), (vblk[:, :, :, :], 0.0), (kblk[:, :, :, :], 0.0), (N1w[:, :, :], 0.0)]
            for i in range(2):
                oth = HALF * (1 - i)
                setup += [(qx[i][oth:oth + HALF, :].bitcast(fp32), 0.0), (kx[i][oth:oth + HALF, :].bitcast(fp32), 0.0),
                          (kx[i][oth:oth + TT, :].bitcast(fp32), 1.0)]
            for n, (what, value) in enumerate(setup):
                pool.memset(what, value).then_inc(cleared, 1)
                pool.wait_ge(cleared, n + 1)
            for b in range(B):
                def norm_step(b, a, s):
                    if s < TT:
                        until(pool, "var_ready", b, a * TT + s + 1)
                        pool.tensor_tensor(rstd[:, s % 2, :], ve[:, s % 2, :], minus_half[:, :],
                                           ALU.pow).then_inc(sem["rstd_ready"], 1)
                        until(pool, "rstd_ready", b, a * TT + s + 1)
                    if s and a < 2:
                        t = s - 1
                        until(pool, "xn_ready", b, a * TT + t + 1)
                        if b + a + t == 0:
                            pool.wait_ge(w_a, 16 * LOADS_A)
                        pool.tensor_tensor(X[:, b, t, :], X[:, b, t, :], rows[:, 1 + 2 * a, :],
                                           ALU.add).then_inc(sem["bias_added"], 1)
                        until(pool, "bias_added", b, a * TT + t + 1)

                if b == 0:
                    for s in range(TT + 1):
                        norm_step(b, 0, s)
                until(pool, "ak_top_ready", b, 1)
                pool.partition_all_reduce(k_max, ak_top, P, ACROSS_MAX).then_inc(sem["k_max_ready"], 1)
                for a in (1, 2):
                    for s in range(TT + 1):
                        norm_step(b, a, s)
                until(pool, "val_v", b, TT * (E3 - 1))
                pool.memset(V3_ones, 1.0).then_inc(sem["v3_ready"], 1)
                for t in range(TT):
                    until(pool, "v3_ready", b, t + 1)
                    pool.tensor_tensor(V3_heads[:, t], V3_heads[:, t],
                                       gtop[:, t, :].rearrange("p (a i) -> p a i", i=2).unsqueeze(3)
                                       .broadcast_to([P, PAIRS3, 2, HD3]), ALU.mult).then_inc(sem["v3_ready"], 1)
                until(pool, "v3_ready", b, TT + 1)
                for e in range(E3):
                    until(pool, "st_ps", b, (H3 - 1 + e // 2 % 2) * NB)
                    until(pool, "v3_ready", b, TT + 1)
                    until(pool, "picks_ready", b, e)
                    pool.tensor_copy(picks(e).rearrange("p (h k) -> p h k", h=H3),
                                     pick_f.rearrange("p (h e) -> p h e", h=H3)[:, :, e:e + 1]
                                     .broadcast_to([P, H3, HD3])).then_inc(sem["picks_ready"], 1)
                if b + 1 < B:
                    until(pool, "picks_ready", b, E3)
                    for s in range(TT + 1):
                        norm_step(b + 1, 0, s)

        @block.scalar
        def _(act):
            def copy(dst, src, name):
                act.activation(dst, src, ACT.Copy).then_inc(sem[name], 1)

            def norm_evac(b, a, t):
                until(act, "xnT_ps", b, a * TT + t + 1)
                copy(xT[:, :, t * P:(t + 1) * P],
                     ps[:, 7 if a else 3, 0:D].rearrange("p (a s) -> p a s", a=DA), "xT_ready")

            def biased(dst, n, bank, col, ready, name, b):
                c, half = n // 2, n % 2
                until(act, ready, b, n + 1)
                act.activation(dst[:, half, c * CH:(c + 1) * CH], ps[:, bank + n % 2, :], ACT.Identity,
                               bias=cols[:, col + half:col + half + 1]).then_inc(sem[name], 1)

            for t in range(TT):
                norm_evac(0, 0, t)
            act.wait_ge(w_a, 16 * LOADS_A)
            act.wait_ge(cleared, 3)
            for bb in range(B):
                act.wait_ge(c2k_ps, bb + 1)
                for a in range(DA):
                    for h in range(4):
                        r = HD2 * h
                        last = act.activation(kblk[r:r + HD2, bb, a, h * SKV:(h + 1) * SKV],
                                              ps[r:r + HD2, a, 0:SKV], ACT.Identity,
                                              bias=cols[r:r + HD2, 6 + a:7 + a])
                last.then_inc(c2k_sb, 1)
            for b in range(B):
                for n in range(2 * NC):
                    biased(kqT, n, 2, 2, "k_ps", "k_sb", b)
                until(act, "k_sb", b, 2 * NC)
                act.activation(kk, kqT, ACT.Square).then_inc(sem["kk_sb"], 1)
                for t in range(TT):
                    until(act, "fk_sub", b, t + 1)
                    act.activation(E1[:, t, :], E1[:, t, :], ACT.Exp).then_inc(sem["e_ready"], 1)
                    if t % TC == TC - 1:
                        for n in range(2 * (t // TC), 2 * (t // TC) + 2):
                            biased(kqT, n, 4, 0, "q_ps", "q_sb", b)

                for s in range(LAST):
                    for a, t in due(s, 0):
                        wide, scale = (H1 * NF, 1.0) if a == 0 else (K2, SCALE2)
                        until(act, "f_sub", b, a * TT + t + 1)
                        act.activation(phi[:, t % 2, 0:wide], phi[:, t % 2, 0:wide], ACT.Exp,
                                       scale=scale).then_inc(sem["f_exp"], 1)
                        if a + t == 0:
                            until(act, "ak_ready", b, 1)
                            act.activation(ak_all, ak_all, ACT.Exp).then_inc(sem["w_ready"], 1)
                    for a, t in due(s, 1):
                        until(act, "fT_ps", b, a * TT + t + 1)
                        if t >= 2:
                            until(act, "num_ps", b, a * TT + t - 1)
                        i = t % 2
                        if a == 0:
                            copy(phT[:, i, :], ps[:, 0:2, :].rearrange("p a s -> p (a s)"), "fT_sb")
                        else:
                            act.activation(phT[:, i, 0:CH], ps[:, 0, :], ACT.Copy)
                            copy(phT[0:K2L, i, CH:CH + P], ps[0:K2L, 1, 0:P], "fT_sb")
                    for a, t in due(s, 3):
                        until(act, "cxT_ps", b, a * TT + t + 1)
                        if t >= 2:
                            until(act, "y_ps", b, a * TT + t - 1)
                        copy(cxT[:, t % 2, :, :], ps[:, 4, 0:D].rearrange("p (a s) -> p a s", a=DA), "cxT_sb")
                    for a, t in due(s, 6):
                        norm_evac(b, a + 1, t)
                        if a == 0 and t % TC == TC - 1:
                            for n in range(2 * (t // TC), 2 * (t // TC) + 2):
                                biased(kqT, n, 2, 4, "q2_ps", "q2_sb", b)
                    if 0 <= (t := s - VALUES_AT) < TT:
                        until(act, "val_ps", b, t + 1)
                        copy(V3_heads[:, t], ps[:, t % 4, :].rearrange("p (a i k) -> p a i k", i=2, k=HD3), "val_a")
                until(act, "gate_ps", b, 1)
                act.activation(g3.rearrange("p t h e -> p (t h e)"), ps[:, 6, :], ACT.Exp,
                               scale=-1.0).then_inc(sem["gate_exp"], 1)
                until(act, "gT_ps", b, 1)
                copy(gT[0:G, :].rearrange("p (i s) -> p i s", i=NC), ps[0:G, 4:4 + NC, :], "gT_a")

                def qk_evac(p, n):
                    i, c = n // NC, n % NC
                    until(act, "qk_ps", b, p * 2 * NC + n + 1)
                    if p and n == 0:
                        until(act, "kst_qx_ready", b, 6 * p)
                        until(act, "kx_ready", b, 2 * p)
                        until(act, "qq_ready", b, 4 * p)
                    act.activation(raw[:, i, c * CH:(c + 1) * CH], ps[:, 6, :], ACT.Copy,
                                   scale=(SCALE3, 1.0)[i]).then_inc(sem["qk_sb"], 1)

                def split(h, k):
                    i, own, oth = h % 2, HALF * (h % 2), HALF * (1 - h % 2)
                    if k == 0:
                        until(act, "qk_sb", b, (h // 2 + 1) * 2 * NC)
                        if h >= 2:
                            until(act, "st_ps", b, (h - 1) * NB)
                        copy(qq[i][own:own + HALF, :], raw[own:own + HALF, 0, :], "qq_ready")
                    elif k == 1:
                        copy(qq[i][oth:oth + HALF, :], raw[own:own + HALF, 0, :], "qq_ready")
                    else:
                        copy(kx[i][own:own + HALF, :], raw[own:own + HALF, 1, :], "kx_ready")

                def evacuate(h, c):
                    own, oth, cs = HALF * (h % 2), HALF * (1 - h % 2), slice(c * CH, (c + 1) * CH)
                    until(act, "av_used", b, h * NB + ENDS[c])
                    if h % 2 == 0 and h:
                        until(act, "oT_ready", b, (h // 2 - 1) * NC + c + 1)
                    copy(oT[own:own + HALF, h // 2, cs], ps[own:own + HALF, SUM_BANK[c], :], "o_sb")
                    copy(rden[own:own + HALF, cs], ps[oth:oth + HALF, SUM_BANK[c], :], "o_sb")

                for n in range(2 * NC):
                    qk_evac(0, n)
                for k in range(3):
                    split(0, k)
                for h in range(H3):
                    for n, (c, j) in enumerate(BLOCKS):
                        lo = max(0, j - TC * c) * P
                        g = h * NB + n
                        until(act, "st_ps", b, g + 1)
                        if g >= RING:
                            until(act, "av_used", b, g - RING + 1)
                        act.activation(PT[:, g % RING, lo:CH], ps[:, 4 + g % 2, 0:CH - lo], ACT.Exp
                                       ).then_inc(sem["pt_ready"], 1)
                        if h + 1 < H3 and n < 3:
                            split(h + 1, n)
                        if n == LAG and h:
                            evacuate(h - 1, 1)
                        if n == ENDS[0] + LAG:
                            evacuate(h, 0)
                        if n in PROJECT_AT and h % 2 == 0 and h + 2 < H3:
                            qk_evac(h // 2 + 1, PROJECT_AT.index(n))
                evacuate(H3 - 1, 1)
                if b + 1 < B:
                    for t in range(TT):
                        norm_evac(b + 1, 0, t)

        @block.vector
        def _(dve):
            steps = [0]

            def step(ins):
                steps[0] += 1
                ins.then_inc(dve_step, 1)
                dve.wait_ge(dve_step, steps[0])

            def norm_stats(b, a, t):
                i = t % 2
                step(dve.bn_stats(st[:, i, :], X[:, b, t, :]))
                step(dve.bn_aggr(mv[:, i, :], st[:, i, :]))
                dve.tensor_scalar(ve[:, i, :], mv[:, i, 1:2], EPS_LN, None, ALU.add).then_inc(sem["var_ready"], 1)

            def norm_apply(b, a, t):
                i, idx = t % 2, a * TT + t
                x = X[:, b, t, :]
                until(dve, "rstd_ready", b, idx + 1)
                if idx >= 2:
                    until(dve, "xnT_ps", b, idx - 1)
                dve.tensor_scalar(xn[:, i, :], x, mv[:, i, 0:1], rstd[:, i, 0:1],
                                  ALU.subtract, ALU.mult).then_inc(sem["xn_ready"], 1)

            dve.wait_ge(x_first, 16)
            for t in range(TT):
                if t == TC:
                    dve.wait_ge(x_second, 16)
                norm_stats(0, 0, t)
                if t:
                    norm_apply(0, 0, t - 1)
            norm_apply(0, 0, TT - 1)
            dve.wait_ge(w_a, 16 * LOADS_A)
            dve.tensor_copy(ident_b[:, :], ident).then_inc(casts, 1)
            dve.tensor_copy(neg[:, :, :], neg_f).then_inc(casts, 1)
            step(dve.memset(v2[:, :, :, HD2:V2W], 1.0))
            for bb in range(B):
                dve.wait_ge(c2v_ps, bb + 1)
                dve.tensor_tensor(v2[:, bb, :, 0:HD2],
                                  ps[0:SKV, 4, 0:D].rearrange("p (h k) -> p h k", h=H2),
                                  rows[0:SKV, 2, :].rearrange("p (h k) -> p h k", h=H2),
                                  ALU.add).then_inc(c2v_sb, 1)
            for b in range(B):
                step(dve.memset(V1_all, 1.0))
                for t in range(TT):
                    until(dve, "v_ps", b, t + 1)
                    dve.tensor_tensor(V1[:, t, :, 0:HD1],
                                      ps[:, 4 + t % 2, 0:D].rearrange("p (h k) -> p h k", h=H1),
                                      rows[:, 0, :].rearrange("p (h k) -> p h k", h=H1),
                                      ALU.add).then_inc(sem["v_sb"], 1)
                for t in range(TT):
                    f = ps[:, 2 - 2 * (t % 2):4 - 2 * (t % 2), :].rearrange("p a (h f) -> p (a h) f", f=NF)
                    until(dve, "fk_ps", b, t + 1)
                    step(dve.tensor_reduce(mk[:, t, :], f, AX.X, ALU.max))
                    if b == 0 and t == 0:
                        dve.wait_ge(v2_placed, 16 * B * len(V2_RUNS))
                    dve.tensor_tensor(E1[:, t, :].rearrange("p (h f) -> p h f", f=NF), f,
                                      mk[:, t, :].unsqueeze(2).broadcast_to([P, H1, NF]),
                                      ALU.subtract).then_inc(sem["fk_sub"], 1)
                until(dve, "kk_ps", b, 1)
                step(dve.scalar_tensor_tensor(ak_all, ps[:, 6, 0:TT * H1], -0.5, mk_all, ALU.mult, ALU.add))
                dve.tensor_reduce(ak_top, ak.rearrange("p t h -> p h t"), AX.X, ALU.max
                                  ).then_inc(sem["ak_top_ready"], 1)

                for s in range(LAST):
                    for a, t in due(s, 0):
                        i = t % 2
                        H = (H1, H2)[a]
                        until(dve, "f_ps", b, a * TT + t + 1)
                        if a == 0:
                            f = ps[:, 2:4, :].rearrange("p a (h f) -> p (a h) f", f=NF)
                            o = phi[:, i, :].rearrange("p (h f) -> p h f", f=NF)
                            m, mb = top[:, i, 0:H], top[:, i, 0:H].unsqueeze(2).broadcast_to([P, H, NF])
                        else:
                            f = ps[:, 2:4, 0:4 * SKV].rearrange("p a (h f) -> p a h f", f=SKV)
                            o = phi[:, i, 0:K2].rearrange("p (a h f) -> p a h f", a=DA, f=SKV)
                            m = top[:, i, 0:H].rearrange("p (a h) -> p a h", a=DA)
                            mb = m.unsqueeze(3).broadcast_to([P, DA, 4, SKV])
                        step(dve.tensor_reduce(m, f, AX.X, ALU.max))
                        if t >= 2:
                            until(dve, "fT_ps", b, a * TT + t - 1)
                        dve.tensor_tensor(o, f, mb, ALU.subtract).then_inc(sem["f_sub"], 1)
                    if s == 0:
                        until(dve, "k_max_ready", b, 1)
                        dve.tensor_tensor(ak, ak, k_max.unsqueeze(1).broadcast_to([P, TT, H1]),
                                          ALU.subtract).then_inc(sem["ak_ready"], 1)
                    if s == 1:
                        until(dve, "w_ready", b, 1)
                        dve.tensor_tensor(V1.rearrange("p t h w -> p (t h) w"), V1.rearrange("p t h w -> p (t h) w"),
                                          ak_all.unsqueeze(2).broadcast_to([P, TT * H1, V1W]),
                                          ALU.mult).then_inc(sem["wv_ready"], 1)
                    if s == 2:
                        until(dve, "n_ps", b, 1)
                        if b == 0:
                            dve.wait_ge(cleared, 4)
                        for k in range(PAIRS1):
                            w0 = k * 2 * V1W - N1_at(k)
                            n1 = ps[:, 4 + k // 4, k % 4 * P:k % 4 * P + 2 * V1W]
                            dve.tensor_copy(N1w[0:HALF, k, w0:w0 + V1W], n1[0:HALF, 0:V1W]
                                            ).then_inc(sem["n_blk"], 1)
                            dve.tensor_copy(N1w[HALF:P, k, w0 + V1W:w0 + 2 * V1W], n1[HALF:P, V1W:2 * V1W]
                                            ).then_inc(sem["n_blk"], 1)
                        until(dve, "za_ps", b, 1)
                        for k0, k1, w0 in N1_RUNS:
                            dens = N1w[:, k0:k1, w0 + HD1:w0 + 2 * V1W:V1W]
                            dve.tensor_tensor(dens, dens, ps[:, 6, 2 * k0:2 * k1].rearrange("p (a i) -> p a i", i=2),
                                              ALU.add).then_inc(sem["n_ready"], 1)
                    for a, t in due(s, 2):
                        i = t % 2
                        H, HD, W = (H1, HD1, V1W) if a == 0 else (H2, HD2, V2W)
                        num = ps[:, 6, 0:H * W].rearrange("p (h w) -> p h w", w=W)
                        until(dve, "num_ps", b, a * TT + t + 1)
                        step(dve.reciprocal(rc[:, i, 0:H], num[:, :, HD]))
                        if t >= 2:
                            until(dve, "cxT_ps", b, a * TT + t - 1)
                        dve.tensor_tensor(cx[:, i, :].rearrange("p (h k) -> p h k", h=H), num[:, :, 0:HD],
                                          rc[:, i, 0:H].unsqueeze(2).broadcast_to([P, H, HD]),
                                          ALU.mult).then_inc(sem["cx_ready"], 1)
                    for a, t in due(s, 5):
                        norm_apply(b, a + 1, t)
                    for a, t in due(s, 4):
                        until(dve, "y_ps", b, a * TT + t + 1)
                        until(dve, "bias_added", b, a * TT + t + 1)
                        step(dve.tensor_tensor(X[:, b, t, :], ps[:, 5, 0:D], X[:, b, t, :], ALU.add))
                        norm_stats(b, a + 1, t)
                g3f, gwf, onef = (v.rearrange("p t h e -> p (t h e)") for v in (g3, gw, one))
                g3h, gwh, oneh, hoth = (v.rearrange("p t h e -> p (t h) e") for v in (g3, gw, one, hot))
                gt, gi = gtop.rearrange("p t h -> p (t h)"), gidx.rearrange("p t h -> p (t h)")
                wide = lambda v: v.unsqueeze(2).broadcast_to([P, TT * H3, E3])
                until(dve, "gate_exp", b, 1)
                step(dve.tensor_scalar(g3f, g3f, 1.0, None, ALU.add))
                step(dve.reciprocal(g3f, g3f))
                step(dve.tensor_reduce(gt, g3h, AX.X, ALU.max))
                step(dve.tensor_tensor(oneh, g3h, wide(gt), ALU.is_equal))
                step(dve.scalar_tensor_tensor(gwh, oneh, -float(E3),
                                              iota_e.unsqueeze(1).broadcast_to([P, TT * H3, E3]),
                                              ALU.mult, ALU.add))
                step(dve.tensor_reduce(gi, gwh, AX.X, ALU.min))
                step(dve.tensor_tensor(hoth, gwh, wide(gi), ALU.is_equal))
                dve.tensor_tensor(gwh, hoth, wide(gt), ALU.mult).then_inc(sem["g_ready"], 1)
                until(dve, "gT_a", b, 1)
                dve.tensor_tensor(gT[G:2 * G, :].rearrange("p (i s) -> p i s", i=NC), ps[0:G, 4:4 + NC, :],
                                  gT[0:G, :].bitcast(fp32).rearrange("p (i s) -> p i s", i=NC),
                                  ALU.subtract).then_inc(sem["gT_v"], 1)
                for n in range(TT, TT * E3):
                    e, t = n // TT, n % TT
                    until(dve, "val_ps", b, n + 1)
                    if e == 1:
                        until(dve, "val_a", b, t + 1)
                    chosen = hot[:, t, :, e].bitcast(u32).rearrange("p (a i) -> p a i", i=2)
                    dve.copy_predicated(V3_heads[:, t], chosen.unsqueeze(3).broadcast_to([P, PAIRS3, 2, HD3]),
                                        ps[:, n % 4, :].rearrange("p (a i k) -> p a i k", i=2, k=HD3)
                                        ).then_inc(sem["val_v"], 1)

                def split(h):
                    i, own, oth = h % 2, HALF * (h % 2), HALF * (1 - h % 2)
                    until(dve, "qk_sb", b, (h // 2 + 1) * 2 * NC)
                    if h >= 2:
                        until(dve, "st_ps", b, (h - 1) * NB)
                    dve.tensor_copy(kst[i][own:own + HALF, :], raw[own:own + HALF, 1, :]
                                    ).then_inc(sem["kst_qx_ready"], 1)
                    until(dve, "kst_qx_ready", b, 3 * h + 1)
                    dve.tensor_tensor(kst[i][oth:oth + HALF, :], raw[own:own + HALF, 1, :],
                                      kst[i][own:own + HALF, :].bitcast(fp32), ALU.subtract
                                      ).then_inc(sem["kst_qx_ready"], 1)
                    until(dve, "qq_ready", b, 2 * h + 1)
                    dve.tensor_tensor(qx[i][own:own + HALF, :], raw[own:own + HALF, 0, :],
                                      qq[i][own:own + HALF, :].bitcast(fp32), ALU.subtract
                                      ).then_inc(sem["kst_qx_ready"], 1)

                def maxima(h):
                    i = h % 2
                    if h >= 2:
                        until(dve, "mxT_ps", b, h - 1)
                    for m, (t, c) in enumerate(SCORES):
                        w = min(CH, (t + 1) * P - c * CH)
                        until(dve, "s_ps", b, h * NB + m + 1)
                        dve.tensor_reduce(mx[:, i, c * TT + t - c * TC:c * TT + t - c * TC + 1],
                                          ps[:, m % MAX_BANKS, 0:w], AX.X, ALU.max).then_inc(sem["s_max"], 1)
                    until(dve, "s_max", b, (h + 1) * NB)
                    dve.tensor_tensor(mx[:, i, TC:TT], mx[:, i, TC:TT], mx[:, i, TT:NB], ALU.max
                                      ).then_inc(sem["tile_max"], 1)

                def max_row(h):
                    i, oth = h % 2, HALF * (1 - h % 2)
                    until(dve, "mxT_ps", b, h + 1)
                    if b == 0 and h < 2:
                        dve.wait_ge(cleared, SETUP)
                    dve.tensor_tensor(qx[i][oth:oth + TT, :].rearrange("p (t s) -> p t s", t=TT),
                                      ps[0:TT, 6, 0:P].unsqueeze(1).broadcast_to([TT, TT, P]),
                                      neg_delta[:, :, :], ALU.mult).then_inc(sem["m_row"], 1)

                def normalise(p, c):
                    cs = slice(c * CH, (c + 1) * CH)
                    until(dve, "o_sb", b, 2 * (NC * (2 * p + 1) + c + 1))
                    step(dve.reciprocal(rden[:, cs], rden[:, cs]))
                    dve.tensor_tensor(oT[:, p, cs], oT[:, p, cs], rden[:, cs], ALU.mult
                                      ).then_inc(sem["oT_ready"], 1)

                for h in range(H3):
                    split(h)
                    maxima(h)
                    max_row(h)
                    if h >= 2:
                        normalise(h // 2 - 1, h % 2)
                for c in range(NC):
                    normalise(PAIRS3 - 1, c)
                until(dve, "oT_ready", b, PAIRS3 * NC)
                for m in range(NC * NEP):
                    n, c = m // NC, m % NC
                    p = n % PAIRS3
                    until(dve, "mask_ps", b, m + 1)
                    if m >= MO:
                        until(dve, "mo_used", b, m - MO + 1)
                    dve.tensor_tensor(mo[:, m % MO, :], ps[:, m % 3, :], oT[:, p, c * CH:(c + 1) * CH],
                                      ALU.mult).then_inc(sem["mo_ready"], 1)
                    if b + 1 < B and m % 6 == 4 and m // 6 <= TT:
                        if m == 4:
                            dve.wait_ge(x_next, 16)
                        if m // 6 < TT:
                            norm_stats(b + 1, 0, m // 6)
                        if m // 6:
                            norm_apply(b + 1, 0, m // 6 - 1)
                until(dve, "mo_used", b, NC * NEP)
                for i in range(TC):
                    dve.tensor_tensor(X[:, b, 2 * i:2 * i + 2, :],
                                      ps[:, 4 + i, :].rearrange("p (t n) -> p t n", t=2),
                                      X[:, b, 2 * i:2 * i + 2, :], ALU.add).then_inc(sem["out_ready"], 1)

        @block.tensor
        def _(pe):
            mm = pe.matmul

            def norm_transpose(b, a, t):
                idx = a * TT + t
                until(pe, "xn_ready", b, idx + 1)
                until(pe, "xT_ready", b, idx)
                for h in range(DA):
                    last = pe.transpose(ps[:, 7 if a else 3, h * P:(h + 1) * P], xn[:, t % 2, h * P:(h + 1) * P], ident)
                last.then_inc(sem["xnT_ps"], 1)

            def values(b, n):
                e, t = n // TT, n % TT
                g = b * PIECES + e
                if t == 0:
                    pe.wait_ge(expert_in[g % SLOTS], 16 * (g // SLOTS + 1))
                if 4 <= n < 4 + TT:
                    until(pe, "val_a", b, n - 3)
                elif n >= 4 + TT:
                    until(pe, "val_v", b, n - 3 - TT)
                for i in range(DA):
                    last = mm(ps[:, n % 4, :], xT[:, i, t * P:(t + 1) * P],
                              experts[:, g % SLOTS, i * HK:(i + 1) * HK], start=(i == 0), stop=(i == DA - 1))
                last.then_inc(sem["val_ps"], 1)

            def projection(n, bank, w, name):
                c, half = n // 2, n % 2
                for i in range(DA):
                    last = mm(ps[:, bank + n % 2, :], w[:, i, half * P:(half + 1) * P],
                              xT[:, i, c * CH:(c + 1) * CH], start=(i == 0), stop=(i == DA - 1))
                last.then_inc(sem[name], 1)

            pe.wait_ge(w_a, 16 * LOADS_A)
            for t in range(TT):
                norm_transpose(0, 0, t)
            pe.wait_ge(w_b, 16 * LOADS_B)
            for bb in range(B):
                if bb:
                    pe.wait_ge(c2k_sb, bb)
                    pe.wait_ge(c2v_sb, bb)
                for a in range(DA):
                    for i in range(2):
                        last = mm(ps[:, a, 0:SKV], W2k[:, i, a * P:(a + 1) * P],
                                  ctxT[:, i, bb * SKV:(bb + 1) * SKV], start=(i == 0), stop=(i == 1))
                last.then_inc(c2k_ps, 1)
                for i in range(2):
                    last = mm(ps[0:SKV, 4, 0:D], ctxT[:, i, bb * SKV:(bb + 1) * SKV], W2v[:, i, :],
                              start=(i == 0), stop=(i == 1))
                last.then_inc(c2v_ps, 1)
            pe.wait_ge(c2v_sb, B)
            pe.wait_ge(c2k_sb, B)
            for b in range(B):
                if b:
                    until(pe, "out_ready", b - 1, TC)
                until(pe, "xT_ready", b, TT)
                for n in range(2 * NC):
                    if n >= 2:
                        until(pe, "k_sb", b, n - 1)
                    projection(n, 2, WkT, "k_ps")
                for t in range(TT):
                    if t >= 2:
                        until(pe, "v_sb", b, t - 1)
                    for i in range(DA):
                        last = mm(ps[:, 4 + t % 2, 0:D], xT[:, i, t * P:(t + 1) * P], WvT[:, i, :],
                                  start=(i == 0), stop=(i == DA - 1))
                    last.then_inc(sem["v_ps"], 1)
                until(pe, "k_sb", b, 2 * NC)
                for t in range(TT):
                    if t == 1:
                        until(pe, "kk_sb", b, 1)
                        for m in range(TT * DA):
                            last = mm(ps[:, 6, m * 8:m * 8 + 96], kk[:, m % DA, m // DA * P:(m // DA + 1) * P],
                                      head_of, start=(m == 0), stop=(m == TT * DA - 1), skip_group_check=True)
                        last.then_inc(sem["kk_ps"], 1)
                    if t >= 2:
                        until(pe, "fk_sub", b, t - 1)
                    for a in range(DA):
                        last = mm(ps[:, 2 - 2 * (t % 2) + a, :], kqT[:, a, t * P:(t + 1) * P], W0[:, a, :],
                                  start=True, stop=True)
                    last.then_inc(sem["fk_ps"], 1)
                    if t % TC == TC - 1:
                        until(pe, "v_sb", b, TT)
                        for n in range(2 * (t // TC), 2 * (t // TC) + 2):
                            if n >= 2:
                                until(pe, "q_sb", b, n - 1)
                            projection(n, 4, WqT, "q_ps")
                until(pe, "q_sb", b, 2 * NC)
                until(pe, "fk_sub", b, TT)

                for s in range(LAST):
                    for a, t in due(s, 0):
                        if a and t == 0:
                            pe.wait_ge(v2_placed, 16 * B * len(V2_RUNS))
                        if a:
                            until(pe, "q2_sb", b, 2 * (TC if s <= TT + 5 else 2 * TC) // TC)
                        until(pe, "f_sub", b, a * TT + t)
                        for i in range(DA):
                            if a == 0:
                                last = mm(ps[:, 2 + i, :], kqT[:, i, t * P:(t + 1) * P], W0[:, i, :],
                                          start=True, stop=True)
                            else:
                                last = mm(ps[:, 2 + i, 0:4 * SKV], kqT[:, i, t * P:(t + 1) * P],
                                          kblk[:, b, i, :], start=True, stop=True)
                        last.then_inc(sem["f_ps"], 1)
                    for a, t in due(s, 1):
                        until(pe, "f_exp", b, a * TT + t + 1)
                        until(pe, "fT_sb", b, a * TT + t)
                        for k in range((PAIRS1, K2C)[a]):
                            r = P if a == 0 else min(P, K2 - k * P)
                            last = pe.transpose(ps[0:r, k // TC, k % TC * P:(k % TC + 1) * P],
                                                phi[:, t % 2, k * P:k * P + r], ident)
                        last.then_inc(sem["fT_ps"], 1)
                    if s == 2:
                        until(pe, "e_ready", b, TT)
                        until(pe, "wv_ready", b, 1)
                        for p in range(PAIRS1):
                            for t in range(TT):
                                c0 = (t * PAIRS1 + p) * 2 * V1W
                                last = mm(ps[:, 4 + p // 4, p % 4 * P:p % 4 * P + WIN], E1[:, t, p * P:(p + 1) * P],
                                          V1_all[:, c0:c0 + WIN], start=(t == 0), stop=(t == TT - 1))
                        last.then_inc(sem["n_ps"], 1)
                        until(pe, "n_blk", b, 2 * PAIRS1)
                        for k0, k1, w0 in N1_RUNS:
                            last = mm(ps[:, 6, 2 * k0:2 * k1], eps_blk,
                                      N1w[:, k0:k1, w0 + HD1:w0 + 2 * V1W:V1W], start=True, stop=True)
                        last.then_inc(sem["za_ps"], 1)
                        until(pe, "n_ready", b, 3)
                    for a, t in due(s, 2):
                        until(pe, "fT_sb", b, a * TT + t + 1)
                        until(pe, "cx_ready", b, a * TT + t)
                        chunks = (PAIRS1, K2C)[a]
                        for k in range(chunks):
                            if a == 0:
                                w0, w, r, src = N1_at(k), WIN, P, N1w[:, k, :]
                            else:
                                w0, w, r = FIRST2[k] * V2W, HEADS2[k] * V2W, min(P, K2 - k * P)
                                src = vblk[0:r, b, k, 0:w]
                            last = mm(ps[:, 6, w0:w0 + w], phT[0:r, t % 2, k * P:(k + 1) * P], src,
                                      start=(k == 0), stop=(k == chunks - 1), skip_group_check=True)
                        last.then_inc(sem["num_ps"], 1)
                    for a, t in due(s, 3):
                        until(pe, "cx_ready", b, a * TT + t + 1)
                        until(pe, "cxT_sb", b, a * TT + t)
                        for h in range(DA):
                            last = pe.transpose(ps[:, 4, h * P:(h + 1) * P], cx[:, t % 2, h * P:(h + 1) * P], ident)
                        last.then_inc(sem["cxT_ps"], 1)
                    for a, t in due(s, 4):
                        until(pe, "cxT_sb", b, a * TT + t + 1)
                        if a + t:
                            until(pe, "var_ready", b, (a + 1) * TT + t)
                        for i in range(DA):
                            last = mm(ps[:, 5, 0:D], cxT[:, t % 2, i, :], (WoT, W2o)[a][:, i, :],
                                      start=(i == 0), stop=(i == DA - 1))
                        last.then_inc(sem["y_ps"], 1)
                    for a, t in due(s, 6):
                        norm_transpose(b, a + 1, t)
                        if a == 0 and t % TC == TC - 1:
                            until(pe, "xT_ready", b, TT + t + 1)
                            until(pe, "f_sub", b, TT + max(0, s - OFFSET[1] + 1))
                            for n in range(2 * (t // TC), 2 * (t // TC) + 2):
                                if n >= 2:
                                    until(pe, "q2_sb", b, n - 1)
                                projection(n, 2, W2q, "q2_ps")
                    if 0 <= (t := s - VALUES_AT) < TT:
                        until(pe, "xT_ready", b, 2 * TT + t + 1)
                        if t == 0:
                            until(pe, "f_sub", b, 2 * TT)
                            until(pe, "fT_sb", b, 2 * TT)
                        values(b, t)

                until(pe, "xT_ready", b, 3 * TT)
                for t in range(TT):
                    w = min(96, CH - t * G)
                    for i in range(DA):
                        last = mm(ps[:, 6, t * G:t * G + w], xT[:, i, t * P:(t + 1) * P], Wg[:, i, 0:w],
                                  start=(t + i == 0), stop=(t == TT - 1 and i == DA - 1), skip_group_check=True)
                last.then_inc(sem["gate_ps"], 1)
                for n in range(TT, TT * E3):
                    if n == TT + 4:
                        until(pe, "g_ready", b, 1)
                        for k in range(TT):
                            last = pe.transpose(ps[0:G, 4 + k // TC, k % TC * P:(k % TC + 1) * P],
                                                gw[:, k, :, :].rearrange("p h e -> p (h e)"), ident)
                        last.then_inc(sem["gT_ps"], 1)
                    values(b, n)

                def project(p, n):
                    w, c = (W3q, W3k)[n // NC], n % NC
                    until(pe, "qk_sb", b, p * 2 * NC + n)
                    if n == 0 and p:
                        until(pe, "m_row", b, 2 * p - 1)
                    for i in range(DA):
                        last = mm(ps[:, 6, :], w[:, i, p * P:(p + 1) * P], xT[:, i, c * CH:(c + 1) * CH],
                                  start=(i == 0), stop=(i == DA - 1))
                    last.then_inc(sem["qk_ps"], 1)

                def scores(h, m):
                    i, (t, c) = h % 2, SCORES[m]
                    if m == 0:
                        until(pe, "qq_ready", b, 2 * h + 2)
                        until(pe, "kst_qx_ready", b, 3 * h + 2)
                    until(pe, "s_max", b, h * NB + m + 1 - MAX_BANKS)
                    w, diagonal = min(CH, (t + 1) * P - c * CH), c == t // TC
                    last = mm(ps[:, m % MAX_BANKS, 0:w], qq[i][:, t * P:(t + 1) * P], kst[i][:, c * CH:c * CH + w],
                              start=True, stop=not diagonal)
                    if diagonal:
                        last = mm(ps[:, m % MAX_BANKS, w - P:w], ident_b[:, :], neg[:, 0, :], start=False, stop=True)
                    last.then_inc(sem["s_ps"], 1)

                def max_rows(h):
                    until(pe, "tile_max", b, h + 1)
                    until(pe, "qk_sb", b, min(PAIRS3, (h + 1) // 2 + 1) * 2 * NC)
                    pe.transpose(ps[0:TT, 6, 0:P], mx[:, h % 2, 0:TT], ident).then_inc(sem["mxT_ps"], 1)

                def weigh(g):
                    h, (c, j) = g // NB, BLOCKS[g % NB]
                    lo = max(0, j - TC * c) * P
                    until(pe, "pt_ready", b, g + 1)
                    if j == 0 and h:
                        until(pe, "o_sb", b, 2 * ((h - 1) * NC + c + 1))
                    mm(ps[:, SUM_BANK[c], lo:CH], V3[:, j, h // 2, h % 2 * HD3:(h % 2 + 2) * HD3],
                       PT[:, g % RING, lo:CH], start=(j == 0), stop=(j == TC * (c + 1) - 1)
                       ).then_inc(sem["av_used"], 1)

                if b == 0:
                    pe.wait_ge(w_c, 16 * 2)
                    pe.wait_ge(casts, 2)
                    pe.wait_ge(cleared, SETUP)
                for n in range(2 * NC):
                    project(0, n)
                until(pe, "val_v", b, TT * (E3 - 1))
                for m in range(NB):
                    scores(0, m)
                max_rows(0)
                until(pe, "v3_ready", b, TT + 1)
                until(pe, "gT_v", b, 1)
                for h in range(H3):
                    i = h % 2
                    until(pe, "kx_ready", b, h + 1)
                    until(pe, "kst_qx_ready", b, 3 * h + 3)
                    until(pe, "m_row", b, h + 1)
                    for n, (c, j) in enumerate(BLOCKS):
                        lo, g = max(0, j - TC * c) * P, h * NB + n
                        w = CH - lo
                        until(pe, "pt_ready", b, g - 1)
                        bank, key, query = 4 + g % 2, slice(j * P, (j + 1) * P), slice(c * CH + lo, (c + 1) * CH)
                        mm(ps[:, bank, 0:w], kst[i][:, key], qq[i][:, query], start=True, stop=False)
                        last = mm(ps[:, bank, 0:w], kx[i][:, key], qx[i][:, query], start=False, stop=j < TC * c)
                        if j >= TC * c:
                            last = mm(ps[:, bank, 0:P], ident_b[:, :], neg[:, 1, :], start=False, stop=True)
                        last.then_inc(sem["st_ps"], 1)
                        if g >= LAG:
                            weigh(g - LAG)
                        if n in PROJECT_AT and h % 2 == 0 and h + 2 < H3:
                            project(h // 2 + 1, PROJECT_AT.index(n))
                        if h + 1 < H3:
                            for m in SCORES_AT.get(n, ()):
                                scores(h + 1, m)
                            if n == MAX_ROW_AT:
                                max_rows(h + 1)
                for g in range(H3 * NB - LAG, H3 * NB):
                    weigh(g)

                def mask(m):
                    n, c = m // NC, m % NC
                    e, p = n // PAIRS3, n % PAIRS3
                    until(pe, "mo_ready", b, m - 2)
                    until(pe, "picks_ready", b, e + 1)
                    mm(ps[:, m % 3, :], picks(e)[:, p * P:(p + 1) * P], gT[:, c * CH:(c + 1) * CH],
                       start=True, stop=True).then_inc(sem["mask_ps"], 1)

                mask(0)
                mask(1)
                until(pe, "o_sb", b, 2 * H3 * NC)
                for m in range(NC * NEP):
                    n, c = m // NC, m % NC
                    e, p = n // PAIRS3, n % PAIRS3
                    g = b * PIECES + E3 + e
                    if m + 2 < NC * NEP:
                        mask(m + 2)
                    if p == 0 and c == 0:
                        pe.wait_ge(expert_in[g % SLOTS], 16 * (g // SLOTS + 1))
                    until(pe, "mo_ready", b, m + 1)
                    for k in range(TC):
                        t = c * TC + k
                        last = mm(ps[:, 4 + t // 2, t % 2 * D:(t % 2 + 1) * D], mo[:, m % MO, k * P:(k + 1) * P],
                                  experts[:, g % SLOTS, p * D:(p + 1) * D], start=(n == 0 and t % 2 == 0),
                                  stop=(n == NEP - 1), skip_group_check=True)
                    last.then_inc(sem["mo_used"], 1)
                    if b + 1 < B and m % 6 == 5 and 1 <= m // 6 <= TT:
                        norm_transpose(b + 1, 0, m // 6 - 1)


def kernel(x, ctx_768, L0_attn_Wq, L0_attn_bq, L0_attn_Wk, L0_attn_bk, L0_attn_Wv, L0_attn_bv, L0_attn_Wo,
           L0_attn_bo, L0_attn_Wrf, L0_xattn_Wq, L0_xattn_bq, L0_xattn_Wk, L0_xattn_bk, L0_xattn_Wv,
           L0_xattn_bv, L0_xattn_Wo, L0_xattn_bo, L0_ffn_w_q, L0_ffn_w_k, L0_ffn_w_gate,
           L0_ffn_value_experts, L0_ffn_output_experts):
    import numpy as np
    import concourse.bacc as bacc
    from concourse.bass_utils import run_bass_kernel_spmd

    P = 128
    arr = lambda a: np.asarray(a)

    def halves(w):
        w = arr(w)
        return w.reshape(w.shape[0] // P, P, -1).transpose(1, 0, 2)

    x, c = arr(x), arr(ctx_768)
    B, S, D = x.shape
    DC = c.shape[2]
    f = x.dtype
    wrf = arr(L0_attn_Wrf)[0]
    H1, HD1, NF = wrf.shape
    w0 = np.zeros((2, 8, HD1, 8, NF), f)
    for h in range(H1):
        w0[h // 8, h % 8, :, h % 8, :] = wrf[h]
    ve, oe = arr(L0_ffn_value_experts), arr(L0_ffn_output_experts)
    E, H, _, K = ve.shape
    ve = ve.reshape(E, H, 2, P, K).transpose(3, 0, 2, 1, 4).reshape(P, E, 2 * H * K)
    oe = oe.reshape(E, H // 2, 2, K, D).transpose(2, 3, 0, 1, 4).reshape(P, E, H // 2 * D)
    two = lambda v: arr(v).reshape(2, P).T
    r, k = np.arange(P)[:, None], np.arange(P)[None, :]
    tri = np.where(k > r, -1e30, 0.0)
    TT = S // P
    const = np.concatenate([
        np.eye(P), np.where(r // NF == k // NF, 1e-6, 0.0), tri, tri.T,
        (r // HD1 == np.arange(96)[None, :]), (r % (H * E) == np.arange(H * E)[None, :]),
        np.tile(np.arange(E)[None, :], (P, 1))], axis=1).astype(f)
    neg_delta = np.zeros((TT, TT, P), f)
    for t in range(TT):
        neg_delta[t, t] = -1.0
    data = {
        "x": x,
        "ctxT": c.reshape(B * c.shape[1], 2, DC // 2).transpose(2, 1, 0),
        "WkT": halves(arr(L0_attn_Wk).T), "WqT": halves(arr(L0_attn_Wq).T),
        "WvT": halves(arr(L0_attn_Wv).T), "WoT": halves(arr(L0_attn_Wo).T),
        "W0": w0.reshape(2, P, 8 * NF).transpose(1, 0, 2),
        "W2q": halves(L0_xattn_Wq), "W2o": halves(L0_xattn_Wo),
        "W2k": arr(L0_xattn_Wk).reshape(2, DC // 2, D).transpose(1, 0, 2),
        "W2v": arr(L0_xattn_Wv).reshape(2, DC // 2, D).transpose(1, 0, 2),
        "Wg": np.concatenate([halves(L0_ffn_w_gate), np.zeros((P, 2, 96 - E * H), f)], axis=2), "W3q": halves(L0_ffn_w_q), "W3k": halves(L0_ffn_w_k),
        "value_experts": ve, "output_experts": oe,
        "cols": np.concatenate([two(L0_attn_bq), two(L0_attn_bk), two(L0_xattn_bq), two(L0_xattn_bk)], axis=1),
        "rows": np.broadcast_to(np.stack([arr(L0_attn_bv), arr(L0_attn_bo), arr(L0_xattn_bv),
                                          arr(L0_xattn_bo)])[None], (P, 4, D)),
        "const": const, "neg_delta": neg_delta,
    }
    nc = bacc.Bacc("TRN2", target_bir_lowering=False, num_devices=1)
    arrays, d = {}, {}
    from concourse import mybir
    for name, a in data.items():
        a = np.ascontiguousarray(a)
        arrays[f"in_{name}"] = a
        d[name] = nc.dram_tensor(f"in_{name}", a.shape, mybir.dt.from_np(a.dtype), kind="ExternalInput").ap()
    out = nc.dram_tensor("out_0", (B, S, D), mybir.dt.from_np(x.dtype), kind="ExternalOutput").ap()
    decoder_layer(nc, d, out)
    got = run_bass_kernel_spmd(nc, [arrays], core_ids=[0])
    return got.results[0]["out_0"]
```

```python
import concourse.bass as bass
from concourse import mybir
from contextlib import ExitStack


def decoder_layer(nc: bass.Bass, d, out: bass.AP):
    fp32 = mybir.dt.float32
    fp32r = mybir.dt.float32r
    bf16 = mybir.dt.bfloat16
    u32 = mybir.dt.uint32
    ALU = mybir.AluOpType
    ACT = mybir.ActivationFunctionType
    AX = mybir.AxisListType
    ACROSS_MAX = bass.bass_isa.ReduceOp.max

    P = 128
    B, S, D = d["x"].shape
    TT = S // P
    CH = 512
    NC = S // CH
    TC = CH // P
    DA = D // P
    HALF = P // 2
    H1, HD1, NF = 16, 16, 64
    V1W = HD1 + 1
    PAIRS1 = H1 // 2
    WIN = 3 * 2 * V1W
    EPS_LN = 1e-5
    H2, HD2 = 8, 32
    DCP, SKV = d["ctxT"].shape[0], d["ctxT"].shape[2] // B
    V2W = HD2 + 1
    K2 = H2 * SKV
    K2C = -(-K2 // P)
    K2L = K2 - (K2C - 1) * P
    FIRST2 = [c * P // SKV for c in range(K2C)]
    HEADS2 = [(min((c + 1) * P, K2) - 1) // SKV + 1 - FIRST2[c] for c in range(K2C)]
    WIDE2 = max(HEADS2) * V2W
    SCALE2 = float(HD2) ** -0.5
    H3, HD3, E3 = 8, 64, 8
    PAIRS3 = H3 // 2
    SCALE3 = float(HD3) ** -0.5
    HK = H3 * HD3
    G = H3 * E3
    BLOCKS = [(c, j) for c in range(NC) for j in range(TC * (c + 1))]
    NB = len(BLOCKS)
    NEP = E3 * PAIRS3
    RING = 4
    LAG = 2
    SLOTS = 2
    AHEAD = 3

    ctx = ExitStack()
    with ctx:
        def sb(name, shape, dt=fp32):
            return ctx.enter_context(nc.sbuf_tensor(name, shape, dt))

        X = sb("X", [P, B, TT, D])
        WkT, WqT, WvT, WoT = (sb(n, [P, DA, D]) for n in ("WkT", "WqT", "WvT", "WoT"))
        W0 = sb("W0", [P, DA, H1 // DA * NF])
        W2q, W2o = sb("W2q", [P, DA, D]), sb("W2o", [P, DA, D])
        Wg = sb("Wg", [P, DA, 96])
        expert = sb("expert", [P, 4 * D])
        expert_hi, expert_lo = (sb(n, [P, SLOTS, 4 * D], fp32r) for n in ("expert_hi", "expert_lo"))
        W3_hi, W3_lo = (sb(n, [P, 2, DA, HK], fp32r) for n in ("W3_hi", "W3_lo"))
        wide_hi, wide_lo = (sb(n, [P, DA, S], fp32r) for n in ("wide_hi", "wide_lo"))
        cols = sb("cols", [P, 8])
        rows = sb("rows", [P, 3, D])
        const = sb("const", [P, 2 * P + 96 + G + E3])
        ident = const[:, 0:P]
        eps_blk = const[:, P:2 * P]
        head_of = const[:, 2 * P:2 * P + 96]
        pick_f = const[:, 2 * P + 96:2 * P + 96 + G]
        iota_e = const[:, 2 * P + 96 + G:]
        ident_b = sb("ident_b", [P, P], bf16)
        neg = sb("neg", [P, 2, P], bf16)
        kblk = sb("kblk", [P, B, DA, 4 * SKV])
        vblk = sb("vblk", [P, B, K2C, WIDE2])
        xT = sb("xT", [P, DA, S])
        xn = sb("xn", [P, 2, D])
        st = sb("st", [P, 2, 6])
        mv = sb("mv", [P, 2, 2])
        ve = sb("ve", [P, 2, 1])
        minus_half = sb("minus_half", [P, 1])
        rstd = sb("rstd", [P, 2, 1])
        top = sb("top", [P, 2, H1])
        rc = sb("rc", [P, 2, H1])
        N1_at = lambda k: min(max(0, k - 1), PAIRS1 - 3) * 2 * V1W

        REGION = 15960
        region = sb("region", [P, REGION])
        at = [0]

        def view(words):
            v = region[:, at[0]:at[0] + words]
            at[0] += words
            assert at[0] <= REGION, at
            return v

        W2k = view(2 * D)[0:DCP].rearrange("p (i n) -> p i n", i=2)
        W2v = view(2 * D)[0:DCP].rearrange("p (i n) -> p i n", i=2)
        ctxT = view(2 * B * SKV)[0:DCP].rearrange("p (i n) -> p i n", i=2)
        v2 = expert[0:SKV, 0:B * H2 * V2W].rearrange("p (b h w) -> p b h w", b=B, h=H2)
        bv2 = view(D)
        neg_f = view(2 * P).rearrange("p (i s) -> p i s", i=2)
        at[0] = 0
        E1 = view(TT * H1 * NF).rearrange("p (t n) -> p t n", t=TT)
        kqT = view(DA * S).rearrange("p (a s) -> p a s", a=DA)
        phi_all = view(2 * H1 * NF)
        phi = phi_all.rearrange("p (i n) -> p i n", i=2)
        kk = phi_all.rearrange("p (a s) -> p a s", a=DA)
        V1_all = view((TT - 1) * H1 * V1W + (PAIRS1 - 1) * 2 * V1W + WIN)
        V1 = V1_all[:, 0:TT * H1 * V1W].rearrange("p (t h w) -> p t h w", t=TT, h=H1)
        mk_all = view(TT * H1)
        mk = mk_all.rearrange("p (t h) -> p t h", t=TT)
        ak_all = view(TT * H1)
        ak = ak_all.rearrange("p (t h) -> p t h", t=TT)
        ak_top = view(H1)
        k_max = view(H1)
        N1w = view(PAIRS1 * WIN).rearrange("p (k w) -> p k w", k=PAIRS1)
        at[0] = 5 * 1024
        cx = view(2 * D).rearrange("p (i n) -> p i n", i=2)
        cxT = view(2 * DA * P).rearrange("p (i a s) -> p i a s", i=2, a=DA)
        phT = view(2 * H1 * NF).rearrange("p (i n) -> p i n", i=2)

        at[0] = 0
        V3 = view(TT * PAIRS3 * 3 * HD3).rearrange("p (t a k) -> p t a k", t=TT, a=PAIRS3)
        V3_heads = V3.rearrange("p t a (i k) -> p t a i k", i=3)[:, :, :, 0:3:2, :]
        V3_ones = V3[:, :, :, HD3:2 * HD3]
        oT = view(PAIRS3 * S).rearrange("p (a s) -> p a s", a=PAIRS3)
        shared = at[0]
        PT = view(RING * CH).rearrange("p (n s) -> p n s", n=RING)
        after = at[0]
        at[0] = shared
        g3, gw, one = (view(TT * G).rearrange("p (t h e) -> p t h e", t=TT, h=H3) for _ in range(3))
        gidx = view(TT * H3).rearrange("p (t h) -> p t h", t=TT)
        at[0] = after
        raw = view(2 * S).rearrange("p (i s) -> p i s", i=2)
        MO = 4
        mo = raw.rearrange("p i (k s) -> p (i k) s", s=CH)
        mo_hi, mo_lo = (v.rearrange("p a (k s) -> p (a k) s", s=CH) for v in (wide_hi[:, :, :], wide_lo[:, :, :]))
        hot = view(TT * G).rearrange("p (t h e) -> p t h e", t=TT, h=H3)
        gtop = view(TT * H3).rearrange("p (t h) -> p t h", t=TT)
        mx = view(2 * NB).rearrange("p (i n) -> p i n", i=2)
        rden = view(S)
        kst, kx, qq, qx = ([sb(f"{n}{i}", [P, S], fp32r) for i in range(2)]
                           for n in ("kst", "kx", "qq", "qx"))
        picks = lambda e: (kst[0], kst[1], qq[0], qq[1])[e // 2][:, e % 2 * HK:(e % 2 + 1) * HK]
        gT = sb("gT", [P, S], fp32r)

        ps = ctx.enter_context(nc.psum_tensor("ps", [P, 8, CH], fp32))

        PER = dict(
            var_ready=3 * TT, rstd_ready=3 * TT, xn_ready=3 * TT, xnT_ps=3 * TT, xT_ready=3 * TT, bias_added=2 * TT,
            k_ps=2 * NC, k_sb=2 * NC, q_ps=2 * NC, q_sb=2 * NC, v_ps=TT, v_sb=TT, kk_sb=1, kk_ps=1,
            fk_ps=TT, fk_sub=TT, e_ready=TT, ak_top_ready=1, k_max_ready=1, ak_ready=1, w_ready=1, wv_ready=1,
            n_ps=2, n_blk=2 * PAIRS1, za_ps=1, n_ready=3,
            f_ps=2 * TT, f_sub=2 * TT, f_exp=2 * TT, fT_ps=2 * TT, fT_sb=2 * TT,
            num_ps=2 * TT, cx_ready=2 * TT, cxT_ps=2 * TT, cxT_sb=2 * TT, y_ps=2 * TT,
            q2_ps=2 * NC, q2_sb=2 * NC,
            gate_ps=NC, gate_exp=NC, g_ready=NC, gT_ps=1, gT_a=1, gT_v=1,
            val_ps=TT * E3, val_a=TT, val_v=TT * (E3 - 1), v3_ready=TT + 1, picks_ready=E3,
            qk_ps=PAIRS3 * 2 * NC, qk_sb=PAIRS3 * 2 * NC,
            qq_ready=2 * H3, kst_ready=2 * H3, qx_ready=H3, kx_ready=H3, o_sb=2 * H3 * NC,
            s_ps=H3 * NB, s_max=H3 * NB, tile_max=H3, mxT_ps=H3, m_row=H3,
            st_ps=H3 * NB, pt_ready=H3 * NB, av_used=H3 * NB, oT_ready=PAIRS3 * NC - 1 + TC,
            mask_ps=NC * NEP, mo_ready=NC * NEP, mo_hi_ready=NC * NEP, mo_lo_ready=NC * NEP,
            x_lo=TT, windows_clear=1, piece_hi=2 * E3, piece_lo=2 * E3, mo_used=NC * NEP, out_ready=TC,
        )
        sem = {n: ctx.enter_context(nc.semaphore(n)) for n in PER}
        (const_in, cols_in, rows_in, kv_in, x_first, x_second, x_next, front_in, later_in, w3_in, expert_in,
         v2_placed, stored, cleared, blocks_clear, casts, w3_hi, w3_lo, c2k_ps, c2v_ps, c2k_sb, c2v_sb, dve_step) = (
            ctx.enter_context(nc.semaphore(n)) for n in (
                "const_in", "cols_in", "rows_in", "kv_in", "x_first", "x_second", "x_next", "front_in", "later_in",
                "w3_in", "expert_in", "v2_placed", "stored", "cleared", "blocks_clear", "casts", "w3_hi", "w3_lo",
                "c2k_ps", "c2v_ps", "c2k_sb", "c2v_sb", "dve_step"))
        block = ctx.enter_context(nc.Block())

        def until(eng, name, b, k):
            if b * PER[name] + k > 0:
                eng.wait_ge(sem[name], b * PER[name] + k)

        SETUP = 7
        LOADS_KV, LOADS_FRONT, LOADS_LATER = 5, 4, 4
        N1_RUNS = [(0, 1, 0), (1, PAIRS1 - 1, 2 * V1W), (PAIRS1 - 1, PAIRS1, 4 * V1W)]
        PIECES = 2 * E3
        V2_RUNS = [(h, max(h * SKV, c * P), min((h + 1) * SKV, (c + 1) * P), c)
                   for c in range(K2C) for h in range(FIRST2[c], FIRST2[c] + HEADS2[c])]

        NEXT_PIECE_AT = {(q - E3 - 1) * PAIRS3 * NC + 2: q for q in range(E3 + SLOTS, PIECES)}
        QUERIES_AT = {3: (0,), 4: (1,), 7: (2, 3)}
        OFFSET = (0, 10)
        VALUES_AT = OFFSET[1] + TT + 1
        LAST = VALUES_AT + TT
        GATES_AT, GATE_BANK = (VALUES_AT + 2, VALUES_AT + 5), (6, 5)
        SCORES = [(t, c) for t in range(TT) for c in range(t // TC + 1)]
        SCORES_AT = {3: (0, 1, 2), 4: (3, 4), 5: (5, 6), 6: (7, 8), 7: (9, 10), 8: (11,)}
        MAX_ROW_AT, MASKS_AT = 9, 9
        PROJECT_AT = (3, 5, 7, 10)
        SUM_BANK = (3, 7)
        MAX_BANKS = 3
        max_bank = lambda h, m: ((4, 5, 7) if h == 0 else (0, 1, 2))[m % MAX_BANKS]
        PROJECT_FIRST, SCORES_FIRST = 4 * TT, 5 * TT + 4
        ENDS = [sum(TC * (k + 1) for k in range(c + 1)) for c in range(NC)]

        def row_bank(b, a, t):
            return 7 if a else 3 if b else 2 + t % 2

        def due(s, lag):
            return [(a, s - OFFSET[a] - lag) for a in range(2) if 0 <= s - OFFSET[a] - lag < TT]

        def piece_used(eng, b, q):
            if q < E3:
                until(eng, "val_ps", b, (q + 1) * TT)
            else:
                until(eng, "mo_used", b, (q - E3 + 1) * PAIRS3 * NC)

        @block.sync
        def _(sp):
            xv = d["x"].rearrange("b (t p) e -> b p t e", p=P)
            ov = out.rearrange("b (t p) e -> b p t e", p=P)
            sp.dma_start(X[:, 0, 0:TC, :], xv[0, :, 0:TC, :]).then_inc(x_first, 16)
            sp.dma_start(const[:, :], d["const"]).then_inc(const_in, 16)
            sp.dma_start(X[:, 0, TC:TT, :], xv[0, :, TC:TT, :]).then_inc(x_second, 16)
            sp.dma_start(rows[:, :, :], d["rows"]).then_inc(rows_in, 16)
            for w, n in ((W2k, "W2k"), (W2v, "W2v"), (ctxT, "ctxT"), (bv2, "bv2"), (neg_f, "neg_f")):
                sp.dma_start(w, d[n]).then_inc(kv_in, 16)
            sp.dma_start(cols[:, :], d["cols"]).then_inc(cols_in, 16)
            for w, n in ((WkT, "WkT"), (WqT, "WqT"), (WvT, "WvT"), (W0, "W0")):
                sp.dma_start(w[:, :, :], d[n]).then_inc(front_in, 16)
            for w, n in ((WoT, "WoT"), (W2q, "W2q"), (W2o, "W2o"), (Wg, "Wg")):
                sp.dma_start(w[:, :, :], d[n]).then_inc(later_in, 16)
            sp.dma_start(X[:, 1, :, :], xv[1]).then_inc(x_next, 16)
            sp.wait_ge(blocks_clear, 2)
            sp.wait_ge(c2v_sb, B)
            for bb in range(B):
                for h, r0, r1, c in V2_RUNS:
                    w0 = (h - FIRST2[c]) * V2W
                    sp.dma_start(vblk[r0 - c * P:r1 - c * P, bb, c, w0:w0 + V2W],
                                 v2[r0 - h * SKV:r1 - h * SKV, bb, h, :]).then_inc(v2_placed, 16)

            sp.wait_ge(v2_placed, 16 * B * len(V2_RUNS))
            sp.dma_start(expert[:, :], d["W3q"]).then_inc(w3_in, 16)
            sp.wait_ge(w3_lo, 1)
            sp.dma_start(expert[:, :], d["W3k"]).then_inc(w3_in, 16)
            sp.wait_ge(w3_lo, 2)
            for b in range(B):
                for q in range(PIECES):
                    g = b * PIECES + q
                    until(sp, "piece_lo", 0, g)
                    sp.dma_start(expert[:, :],
                                 d["value_experts" if q < E3 else "output_experts"][:, q % E3, :]
                                 ).then_inc(expert_in, 16)
                for i in range(TC):
                    until(sp, "out_ready", b, i + 1)
                    sp.dma_start(ov[b, :, 2 * i:2 * i + 2, :], X[:, b, 2 * i:2 * i + 2, :]).then_inc(stored, 16)
            sp.wait_ge(stored, B * TC * 16)

        @block.gpsimd
        def _(pool):
            cleared_so_far = [0]

            def clear(what, value):
                pool.memset(what, value).then_inc(cleared, 1)
                cleared_so_far[0] += 1
                pool.wait_ge(cleared, cleared_so_far[0])

            clear(minus_half[:, :], -0.5)

            def piece_low(b, q):
                g = b * PIECES + q
                until(pool, "piece_hi", b, q + 1)
                pool.tensor_tensor(expert_lo[:, g % SLOTS, :], expert[:, :],
                                   expert_hi[:, g % SLOTS, :].bitcast(fp32), ALU.subtract
                                   ).then_inc(sem["piece_lo"], 1)
                until(pool, "piece_lo", b, q + 1)

            def queries_low(b, h):
                i, own = h % 2, HALF * (h % 2)
                until(pool, "qq_ready", b, 2 * h + 1)
                if h >= 2:
                    until(pool, "st_ps", b, (h - 1) * NB)
                pool.tensor_tensor(qx[i][own:own + HALF, :], raw[own:own + HALF, 0, :],
                                   qq[i][own:own + HALF, :].bitcast(fp32), ALU.subtract
                                   ).then_inc(sem["qx_ready"], 1)
                until(pool, "qx_ready", b, h + 1)

            for b in range(B):
                def rstd_of(b, a, t):
                    until(pool, "var_ready", b, a * TT + t + 1)
                    pool.tensor_tensor(rstd[:, t % 2, :], ve[:, t % 2, :], minus_half[:, :],
                                       ALU.pow).then_inc(sem["rstd_ready"], 1)
                    until(pool, "rstd_ready", b, a * TT + t + 1)

                def add_bias(b, a, t):
                    until(pool, "xn_ready", b, a * TT + t + 1)
                    if b + a + t == 0:
                        pool.wait_ge(rows_in, 16)
                    pool.tensor_tensor(X[:, b, t, :], X[:, b, t, :], rows[:, 1 + a, :],
                                       ALU.add).then_inc(sem["bias_added"], 1)
                    until(pool, "bias_added", b, a * TT + t + 1)

                def norm_step(b, a, s):
                    if s < TT:
                        rstd_of(b, a, s)
                    if s and a < 2:
                        add_bias(b, a, s - 1)

                if b == 0:
                    for t in range(TT):
                        rstd_of(b, 0, t)
                    for t in range(TT):
                        add_bias(b, 0, t)
                    for i in range(2):
                        oth = HALF * (1 - i)
                        clear(qx[i][oth:oth + HALF, :].bitcast(fp32), 0.0)
                        clear(kx[i][oth:oth + HALF, :].bitcast(fp32), 0.0)
                        clear(kx[i][oth:oth + TT, :].bitcast(fp32), 1.0)
                until(pool, "oT_ready", b, 0)
                pool.memset(N1w, 0.0).then_inc(sem["windows_clear"], 1)
                until(pool, "windows_clear", b, 1)
                if b == 0:
                    for i in range(2):
                        pool.wait_ge(w3_hi, i + 1)
                        pool.tensor_tensor(W3_lo[:, i].rearrange("p a n -> p (a n)"), expert[:, :],
                                           W3_hi[:, i].rearrange("p a n -> p (a n)").bitcast(fp32), ALU.subtract
                                           ).then_inc(w3_lo, 1)
                        pool.wait_ge(w3_lo, i + 1)
                until(pool, "ak_top_ready", b, 1)
                pool.partition_all_reduce(k_max, ak_top, P, ACROSS_MAX).then_inc(sem["k_max_ready"], 1)
                for q in range(SLOTS):
                    piece_low(b, q)
                for a in (1, 2):
                    for s in range(TT + 1):
                        norm_step(b, a, s)
                pool.memset(V3_ones, 1.0).then_inc(sem["v3_ready"], 1)
                until(pool, "v3_ready", b, 1)
                for q in range(SLOTS, E3 + 1):
                    piece_low(b, q)
                    if q == PROJECT_FIRST // TT + 1:
                        queries_low(b, 0)
                for t in range(TT):
                    until(pool, "val_v", b, TT * (E3 - 2) + t + 1)
                    pool.tensor_tensor(V3_heads[:, t], V3_heads[:, t],
                                       gtop[:, t, :].rearrange("p (a i) -> p a i", i=2).unsqueeze(3)
                                       .broadcast_to([P, PAIRS3, 2, HD3]), ALU.mult).then_inc(sem["v3_ready"], 1)
                    until(pool, "v3_ready", b, t + 2)
                piece_low(b, E3 + 1)
                for h in range(1, H3):
                    queries_low(b, h)
                for e in range(E3):
                    until(pool, "st_ps", b, (H3 - 1 + e // 2 % 2) * NB)
                    until(pool, "picks_ready", b, e)
                    pool.tensor_copy(picks(e).rearrange("p (h k) -> p h k", h=H3),
                                     pick_f.rearrange("p (h e) -> p h e", h=H3)[:, :, e:e + 1]
                                     .broadcast_to([P, H3, HD3])).then_inc(sem["picks_ready"], 1)
                until(pool, "picks_ready", b, E3)
                for m in range(NC * NEP):
                    if m in NEXT_PIECE_AT:
                        piece_low(b, NEXT_PIECE_AT[m])
                    if b + 1 < B and m % 6 == 4 and m // 6 <= TT:
                        norm_step(b + 1, 0, m // 6)

        @block.scalar
        def _(act):
            def copy(dst, src, name):
                act.activation(dst, src, ACT.Copy).then_inc(sem[name], 1)

            def norm_evac(b, a, t):
                until(act, "xnT_ps", b, a * TT + t + 1)
                if a == 2:
                    act.activation(wide_hi[:, :, t * P:(t + 1) * P],
                                   ps[:, 7, 0:D].rearrange("p (a s) -> p a s", a=DA), ACT.Copy)
                copy(xT[:, :, t * P:(t + 1) * P],
                     ps[:, row_bank(b, a, t), 0:D].rearrange("p (a s) -> p a s", a=DA), "xT_ready")

            def biased(dst, n, bank, col, ready, name, b):
                c, half = n // 2, n % 2
                until(act, ready, b, n + 1)
                act.activation(dst[:, half, c * CH:(c + 1) * CH], ps[:, bank + n % 2, :], ACT.Identity,
                               bias=cols[:, col + half:col + half + 1]).then_inc(sem[name], 1)

            def piece_high(b, q):
                g = b * PIECES + q
                act.wait_ge(expert_in, 16 * (g + 1))
                if g >= SLOTS:
                    piece_used(act, (g - SLOTS) // PIECES, (g - SLOTS) % PIECES)
                copy(expert_hi[:, g % SLOTS, :], expert[:, :], "piece_hi")

            for t in range(TT):
                norm_evac(0, 0, t)
            act.wait_ge(cols_in, 16)
            act.wait_ge(blocks_clear, 2)
            act.wait_ge(c2k_ps, 1)
            for bb in range(B):
                for a in range(DA):
                    for h in range(4):
                        r = HD2 * h
                        last = act.activation(kblk[r:r + HD2, bb, a, h * SKV:(h + 1) * SKV],
                                              ps[r:r + HD2, a, bb * SKV:(bb + 1) * SKV], ACT.Identity,
                                              bias=cols[r:r + HD2, 6 + a:7 + a])
                last.then_inc(c2k_sb, 1)
            for b in range(B):
                for n in range(2 * NC):
                    biased(kqT, n, 2, 2, "k_ps", "k_sb", b)
                until(act, "k_sb", b, 2 * NC)
                act.activation(kk, kqT, ACT.Square).then_inc(sem["kk_sb"], 1)
                for t in range(TT):
                    for n in QUERIES_AT.get(t, ()):
                        biased(kqT, n, 7 - n % 2, 0, "q_ps", "q_sb", b)
                    until(act, "fk_sub", b, t + 1)
                    act.activation(E1[:, t, :], E1[:, t, :], ACT.Exp).then_inc(sem["e_ready"], 1)
                    if b == 0 and t in (1, 4):
                        i = t // 4
                        act.wait_ge(w3_in, 16 * (i + 1))
                        act.activation(W3_hi[:, i].rearrange("p a n -> p (a n)"), expert[:, :], ACT.Copy
                                       ).then_inc(w3_hi, 1)

                def gates(c):
                    until(act, "gate_ps", b, c + 1)
                    act.activation(g3[:, c * TC:(c + 1) * TC].rearrange("p t h e -> p (t h e)"),
                                   ps[:, GATE_BANK[c], 0:TC * G], ACT.Exp, scale=-1.0).then_inc(sem["gate_exp"], 1)

                until(act, "ak_ready", b, 1)
                act.activation(ak_all, ak_all, ACT.Exp).then_inc(sem["w_ready"], 1)
                for s in range(LAST):
                    if s in (2, 3):
                        piece_high(b, s - 2)
                    for a, t in due(s, 1):
                        until(act, "fT_ps", b, a * TT + t + 1)
                        if a + t == 0:
                            until(act, "n_ps", b, 2)
                        if t >= 2:
                            until(act, "num_ps", b, a * TT + t - 1)
                        i = t % 2
                        if a == 0:
                            copy(phT[:, i, :], ps[:, 0:2, :].rearrange("p a s -> p (a s)"), "fT_sb")
                        else:
                            act.activation(phT[:, i, 0:CH], ps[:, 0, :], ACT.Copy)
                            copy(phT[0:K2L, i, CH:CH + P], ps[0:K2L, 1, 0:P], "fT_sb")
                    for a, t in due(s, 0):
                        wide, scale = (H1 * NF, 1.0) if a == 0 else (K2, SCALE2)
                        until(act, "f_sub", b, a * TT + t + 1)
                        act.activation(phi[:, t % 2, 0:wide], phi[:, t % 2, 0:wide], ACT.Exp,
                                       scale=scale).then_inc(sem["f_exp"], 1)
                    for a, t in due(s, 3):
                        until(act, "cxT_ps", b, a * TT + t + 1)
                        if t >= 2:
                            until(act, "y_ps", b, a * TT + t - 1)
                        copy(cxT[:, t % 2, :, :], ps[:, 4, 0:D].rearrange("p (a s) -> p a s", a=DA), "cxT_sb")
                    for a, t in due(s, 6):
                        norm_evac(b, a + 1, t)
                        if a == 0 and t % TC == TC - 1:
                            for n in range(2 * (t // TC), 2 * (t // TC) + 2):
                                biased(kqT, n, 2, 4, "q2_ps", "q2_sb", b)
                    if s in GATES_AT:
                        gates(GATES_AT.index(s))
                    if 0 <= (t := s - VALUES_AT) < TT:
                        until(act, "val_ps", b, t + 1)
                        copy(V3_heads[:, t], ps[:, t % 4, :].rearrange("p (a i k) -> p a i k", i=2, k=HD3), "val_a")
                until(act, "gT_ps", b, 1)
                copy(gT[0:G, :].rearrange("p (i s) -> p i s", i=NC), ps[0:G, 4:4 + NC, :], "gT_a")

                def qk_evac(p, n):
                    i, c = n // NC, n % NC
                    until(act, "qk_ps", b, p * 2 * NC + n + 1)
                    if p and n == 0:
                        until(act, "kst_ready", b, 4 * p)
                        until(act, "qx_ready", b, 2 * p)
                        until(act, "kx_ready", b, 2 * p)
                        until(act, "qq_ready", b, 4 * p)
                    act.activation(raw[:, i, c * CH:(c + 1) * CH], ps[:, 6, :], ACT.Copy,
                                   scale=(SCALE3, 1.0)[i]).then_inc(sem["qk_sb"], 1)

                def split(h, k):
                    i, own, oth = h % 2, HALF * (h % 2), HALF * (1 - h % 2)
                    if k == 0:
                        until(act, "qk_sb", b, (h // 2 + 1) * 2 * NC)
                        if h >= 2:
                            until(act, "st_ps", b, (h - 1) * NB)
                        copy(qq[i][own:own + HALF, :], raw[own:own + HALF, 0, :], "qq_ready")
                    elif k == 1:
                        copy(qq[i][oth:oth + HALF, :], raw[own:own + HALF, 0, :], "qq_ready")
                    else:
                        copy(kx[i][own:own + HALF, :], raw[own:own + HALF, 1, :], "kx_ready")

                def masked_high(m):
                    until(act, "mo_ready", b, m + 1)
                    if m >= MO:
                        until(act, "mo_used", b, m - MO + 1)
                    copy(mo_hi[:, m % MO, :], mo[:, m % MO, :], "mo_hi_ready")

                def evacuate(h, c):
                    own, oth, cs = HALF * (h % 2), HALF * (1 - h % 2), slice(c * CH, (c + 1) * CH)
                    until(act, "av_used", b, h * NB + ENDS[c])
                    if h % 2 == 0 and h:
                        until(act, "oT_ready", b, (h // 2 - 1) * NC + c + 1)
                    copy(oT[own:own + HALF, h // 2, cs], ps[own:own + HALF, SUM_BANK[c], :], "o_sb")
                    copy(rden[own:own + HALF, cs], ps[oth:oth + HALF, SUM_BANK[c], :], "o_sb")

                for q in range(SLOTS, E3 + SLOTS):
                    piece_high(b, q)
                    if q == PROJECT_FIRST // TT + 1:
                        for n in range(2 * NC):
                            qk_evac(0, n)
                        for k in range(3):
                            split(0, k)
                for h in range(H3):
                    for n, (c, j) in enumerate(BLOCKS):
                        lo = max(0, j - TC * c) * P
                        g = h * NB + n
                        until(act, "st_ps", b, g + 1)
                        if g >= RING:
                            until(act, "av_used", b, g - RING + 1)
                        act.activation(PT[:, g % RING, lo:CH], ps[:, 4 + g % 2, 0:CH - lo], ACT.Exp
                                       ).then_inc(sem["pt_ready"], 1)
                        if h + 1 < H3 and n < 3:
                            split(h + 1, n)
                        if h + 1 == H3 and n == MASKS_AT + 1:
                            masked_high(0)
                        if n == LAG and h:
                            evacuate(h - 1, 1)
                        if n == ENDS[0] + LAG:
                            evacuate(h, 0)
                        if n in PROJECT_AT and h % 2 == 0 and h + 2 < H3:
                            qk_evac(h // 2 + 1, PROJECT_AT.index(n))
                evacuate(H3 - 1, 1)
                for m in range(NC * NEP):
                    if m:
                        masked_high(m)
                    if m in NEXT_PIECE_AT:
                        piece_high(b, NEXT_PIECE_AT[m])
                    if b + 1 < B and m % 6 == 5 and 1 <= m // 6 <= TT:
                        norm_evac(b + 1, 0, m // 6 - 1)

        @block.vector
        def _(dve):
            steps = [0]

            def step(ins):
                steps[0] += 1
                ins.then_inc(dve_step, 1)
                dve.wait_ge(dve_step, steps[0])

            def norm_stats(b, a, t):
                i = t % 2
                step(dve.bn_stats(st[:, i, :], X[:, b, t, :]))
                step(dve.bn_aggr(mv[:, i, :], st[:, i, :]))
                dve.tensor_scalar(ve[:, i, :], mv[:, i, 1:2], EPS_LN, None, ALU.add).then_inc(sem["var_ready"], 1)

            def norm_apply(b, a, t):
                i, idx = t % 2, a * TT + t
                x = X[:, b, t, :]
                until(dve, "rstd_ready", b, idx + 1)
                if idx >= 2:
                    until(dve, "xnT_ps", b, idx - 1)
                dve.tensor_scalar(xn[:, i, :], x, mv[:, i, 0:1], rstd[:, i, 0:1],
                                  ALU.subtract, ALU.mult).then_inc(sem["xn_ready"], 1)

            dve.memset(kblk[:, :, :, :], 0.0).then_inc(blocks_clear, 1)
            dve.memset(vblk[:, :, :, :], 0.0).then_inc(blocks_clear, 1)
            dve.wait_ge(x_first, 16)
            for t in range(TT):
                if t == TC:
                    dve.wait_ge(x_second, 16)
                norm_stats(0, 0, t)
                if t:
                    norm_apply(0, 0, t - 1)
            norm_apply(0, 0, TT - 1)
            dve.wait_ge(const_in, 16)
            dve.wait_ge(kv_in, 16 * LOADS_KV)
            dve.tensor_copy(ident_b[:, :], ident).then_inc(casts, 1)
            dve.tensor_copy(neg[:, :, :], neg_f).then_inc(casts, 1)
            step(dve.memset(v2[:, :, :, HD2:V2W], 1.0))
            for bb in range(B):
                dve.wait_ge(c2v_ps, bb + 1)
                dve.tensor_tensor(v2[:, bb, :, 0:HD2],
                                  ps[0:SKV, 6 + bb, 0:D].rearrange("p (h k) -> p h k", h=H2),
                                  bv2[0:SKV].rearrange("p (h k) -> p h k", h=H2),
                                  ALU.add).then_inc(c2v_sb, 1)
            for b in range(B):
                step(dve.memset(V1_all, 1.0))
                for t in range(TT):
                    f = ps[:, 2 - 2 * (t % 2):4 - 2 * (t % 2), :].rearrange("p a (h f) -> p (a h) f", f=NF)
                    until(dve, "fk_ps", b, t + 1)
                    step(dve.tensor_reduce(mk[:, t, :], f, AX.X, ALU.max))
                    dve.tensor_tensor(E1[:, t, :].rearrange("p (h f) -> p h f", f=NF), f,
                                      mk[:, t, :].unsqueeze(2).broadcast_to([P, H1, NF]),
                                      ALU.subtract).then_inc(sem["fk_sub"], 1)
                    until(dve, "v_ps", b, t + 1)
                    dve.tensor_tensor(V1[:, t, :, 0:HD1],
                                      ps[:, 4 + t % 2, 0:D].rearrange("p (h k) -> p h k", h=H1),
                                      rows[:, 0, :].rearrange("p (h k) -> p h k", h=H1),
                                      ALU.add).then_inc(sem["v_sb"], 1)
                until(dve, "kk_ps", b, 1)
                step(dve.scalar_tensor_tensor(ak_all, ps[:, 6, 0:TT * H1], -0.5, mk_all, ALU.mult, ALU.add))
                dve.tensor_reduce(ak_top, ak.rearrange("p t h -> p h t"), AX.X, ALU.max
                                  ).then_inc(sem["ak_top_ready"], 1)

                def gates(c):
                    ts = slice(c * TC, (c + 1) * TC)
                    g3f = g3[:, ts].rearrange("p t h e -> p (t h e)")
                    g3h, gwh, oneh, hoth = (v[:, ts].rearrange("p t h e -> p (t h) e") for v in (g3, gw, one, hot))
                    gt, gi = gtop[:, ts].rearrange("p t h -> p (t h)"), gidx[:, ts].rearrange("p t h -> p (t h)")
                    each = lambda v: v.unsqueeze(2).broadcast_to([P, TC * H3, E3])
                    until(dve, "gate_exp", b, c + 1)
                    step(dve.tensor_scalar(g3f, g3f, 1.0, None, ALU.add))
                    step(dve.reciprocal(g3f, g3f))
                    step(dve.tensor_reduce(gt, g3h, AX.X, ALU.max))
                    step(dve.tensor_tensor(oneh, g3h, each(gt), ALU.is_equal))
                    step(dve.scalar_tensor_tensor(gwh, oneh, -float(E3),
                                                  iota_e.unsqueeze(1).broadcast_to([P, TC * H3, E3]),
                                                  ALU.mult, ALU.add))
                    step(dve.tensor_reduce(gi, gwh, AX.X, ALU.min))
                    step(dve.tensor_tensor(hoth, gwh, each(gi), ALU.is_equal))
                    dve.tensor_tensor(gwh, hoth, each(gt), ALU.mult).then_inc(sem["g_ready"], 1)

                until(dve, "k_max_ready", b, 1)
                dve.tensor_tensor(ak, ak, k_max.unsqueeze(1).broadcast_to([P, TT, H1]),
                                  ALU.subtract).then_inc(sem["ak_ready"], 1)
                until(dve, "w_ready", b, 1)
                dve.tensor_tensor(V1.rearrange("p t h w -> p (t h) w"), V1.rearrange("p t h w -> p (t h) w"),
                                  ak_all.unsqueeze(2).broadcast_to([P, TT * H1, V1W]),
                                  ALU.mult).then_inc(sem["wv_ready"], 1)
                for s in range(LAST):
                    if s - 2 in GATES_AT:
                        gates(GATES_AT.index(s - 2))
                    if s == 2:
                        until(dve, "za_ps", b, 1)
                        for k0, k1, w0 in N1_RUNS:
                            dens = N1w[:, k0:k1, w0 + HD1:w0 + 2 * V1W:V1W]
                            dve.tensor_tensor(dens, dens, ps[:, 6, 2 * k0:2 * k1].rearrange("p (a i) -> p a i", i=2),
                                              ALU.add).then_inc(sem["n_ready"], 1)
                    for a, t in due(s, 0):
                        i = t % 2
                        H = (H1, H2)[a]
                        until(dve, "f_ps", b, a * TT + t + 1)
                        if a == 0:
                            f = ps[:, 2:4, :].rearrange("p a (h f) -> p (a h) f", f=NF)
                            o = phi[:, i, :].rearrange("p (h f) -> p h f", f=NF)
                            m, mb = top[:, i, 0:H], top[:, i, 0:H].unsqueeze(2).broadcast_to([P, H, NF])
                        else:
                            f = ps[:, 2:4, 0:4 * SKV].rearrange("p a (h f) -> p a h f", f=SKV)
                            o = phi[:, i, 0:K2].rearrange("p (a h f) -> p a h f", a=DA, f=SKV)
                            m = top[:, i, 0:H].rearrange("p (a h) -> p a h", a=DA)
                            mb = m.unsqueeze(3).broadcast_to([P, DA, 4, SKV])
                        step(dve.tensor_reduce(m, f, AX.X, ALU.max))
                        if t >= 2:
                            until(dve, "fT_ps", b, a * TT + t - 1)
                        dve.tensor_tensor(o, f, mb, ALU.subtract).then_inc(sem["f_sub"], 1)
                    if s == 1:
                        until(dve, "n_ps", b, 2)
                        until(dve, "windows_clear", b, 1)
                        for k in range(PAIRS1):
                            w0 = k * 2 * V1W - N1_at(k)
                            n1 = ps[:, 4 + k // 4, k % 4 * P:k % 4 * P + 2 * V1W]
                            dve.tensor_copy(N1w[0:HALF, k, w0:w0 + V1W], n1[0:HALF, 0:V1W]
                                            ).then_inc(sem["n_blk"], 1)
                            dve.tensor_copy(N1w[HALF:P, k, w0 + V1W:w0 + 2 * V1W], n1[HALF:P, V1W:2 * V1W]
                                            ).then_inc(sem["n_blk"], 1)
                    for a, t in due(s, 2):
                        i = t % 2
                        H, HD, W = (H1, HD1, V1W) if a == 0 else (H2, HD2, V2W)
                        num = ps[:, 6, 0:H * W].rearrange("p (h w) -> p h w", w=W)
                        until(dve, "num_ps", b, a * TT + t + 1)
                        step(dve.reciprocal(rc[:, i, 0:H], num[:, :, HD]))
                        if t >= 2:
                            until(dve, "cxT_ps", b, a * TT + t - 1)
                        dve.tensor_tensor(cx[:, i, :].rearrange("p (h k) -> p h k", h=H), num[:, :, 0:HD],
                                          rc[:, i, 0:H].unsqueeze(2).broadcast_to([P, H, HD]),
                                          ALU.mult).then_inc(sem["cx_ready"], 1)
                    for a, t in due(s, 5):
                        norm_apply(b, a + 1, t)
                    for a, t in due(s, 7):
                        if a:
                            cs = slice(t * P, (t + 1) * P)
                            until(dve, "xT_ready", b, 2 * TT + t + 1)
                            dve.tensor_tensor(wide_lo[:, :, cs], xT[:, :, cs], wide_hi[:, :, cs].bitcast(fp32),
                                              ALU.subtract).then_inc(sem["x_lo"], 1)
                    for a, t in due(s, 4):
                        until(dve, "y_ps", b, a * TT + t + 1)
                        until(dve, "bias_added", b, a * TT + t + 1)
                        step(dve.tensor_tensor(X[:, b, t, :], ps[:, 5, 0:D], X[:, b, t, :], ALU.add))
                        norm_stats(b, a + 1, t)
                until(dve, "gT_a", b, 1)
                dve.tensor_tensor(gT[G:2 * G, :].rearrange("p (i s) -> p i s", i=NC), ps[0:G, 4:4 + NC, :],
                                  gT[0:G, :].bitcast(fp32).rearrange("p (i s) -> p i s", i=NC),
                                  ALU.subtract).then_inc(sem["gT_v"], 1)
                def split(h):
                    i, own, oth = h % 2, HALF * (h % 2), HALF * (1 - h % 2)
                    until(dve, "qk_sb", b, (h // 2 + 1) * 2 * NC)
                    if h >= 2:
                        until(dve, "st_ps", b, (h - 1) * NB)
                    dve.tensor_copy(kst[i][own:own + HALF, :], raw[own:own + HALF, 1, :]
                                    ).then_inc(sem["kst_ready"], 1)
                    until(dve, "kst_ready", b, 2 * h + 1)
                    dve.tensor_tensor(kst[i][oth:oth + HALF, :], raw[own:own + HALF, 1, :],
                                      kst[i][own:own + HALF, :].bitcast(fp32), ALU.subtract
                                      ).then_inc(sem["kst_ready"], 1)

                def maximum(h, m):
                    i, (t, c) = h % 2, SCORES[m]
                    if h >= 2 and m == 0:
                        until(dve, "mxT_ps", b, h - 1)
                    w, at_mx = min(CH, (t + 1) * P - c * CH), t + c * (TT - TC)
                    until(dve, "s_ps", b, h * NB + m + 1)
                    dve.tensor_reduce(mx[:, i, at_mx:at_mx + 1], ps[:, max_bank(h, m), 0:w], AX.X, ALU.max
                                      ).then_inc(sem["s_max"], 1)
                    if m == NB - 1:
                        until(dve, "s_max", b, (h + 1) * NB)
                        dve.tensor_tensor(mx[:, i, TC:TT], mx[:, i, TC:TT], mx[:, i, TT:NB], ALU.max
                                          ).then_inc(sem["tile_max"], 1)

                def max_row(h):
                    i, oth = h % 2, HALF * (1 - h % 2)
                    until(dve, "mxT_ps", b, h + 1)
                    if b == 0 and h < 2:
                        dve.wait_ge(cleared, SETUP)
                    dve.scalar_tensor_tensor(qx[i][oth:oth + TT, :].rearrange("p (t s) -> p t s", t=TT),
                                             ps[0:TT, 6, 0:P].unsqueeze(1).broadcast_to([TT, TT, P]), -1.0,
                                             ident[0:TT, 0:TT].unsqueeze(2).broadcast_to([TT, TT, P]),
                                             ALU.mult, ALU.mult).then_inc(sem["m_row"], 1)

                def normalise(p, c, k=0, parts=1):
                    cs = slice(c * CH + k * CH // parts, c * CH + (k + 1) * CH // parts)
                    until(dve, "o_sb", b, 2 * (NC * (2 * p + 1) + c + 1))
                    step(dve.reciprocal(rden[:, cs], rden[:, cs]))
                    dve.tensor_tensor(oT[:, p, cs], oT[:, p, cs], rden[:, cs], ALU.mult
                                      ).then_inc(sem["oT_ready"], 1)

                for n in range(TT, TT * E3):
                    e, t = n // TT, n % TT
                    until(dve, "val_ps", b, n + 1)
                    if e == 1:
                        until(dve, "val_a", b, t + 1)
                    chosen = hot[:, t, :, e].bitcast(u32).rearrange("p (a i) -> p a i", i=2)
                    dve.copy_predicated(V3_heads[:, t], chosen.unsqueeze(3).broadcast_to([P, PAIRS3, 2, HD3]),
                                        ps[:, n % 4, :].rearrange("p (a i k) -> p a i k", i=2, k=HD3)
                                        ).then_inc(sem["val_v"], 1)
                    if n == PROJECT_FIRST + TT:
                        split(0)
                    if 0 <= n - SCORES_FIRST < NB:
                        maximum(0, n - SCORES_FIRST)
                    if n == SCORES_FIRST + NB + 1:
                        max_row(0)
                for h in range(1, H3):
                    split(h)
                    for m in range(NB):
                        maximum(h, m)
                    max_row(h)
                    if h >= 2:
                        normalise(h // 2 - 1, h % 2)
                normalise(PAIRS3 - 1, 0)

                def masked(m):
                    p, c = m // NC % PAIRS3, m % NC
                    until(dve, "mask_ps", b, m + 1)
                    if m >= MO:
                        until(dve, "mo_lo_ready", b, m - MO + 1)
                    dve.tensor_tensor(mo[:, m % MO, :], ps[:, m % AHEAD, :], oT[:, p, c * CH:(c + 1) * CH],
                                      ALU.mult).then_inc(sem["mo_ready"], 1)

                until(dve, "oT_ready", b, PAIRS3 * NC - 1)
                until(dve, "kx_ready", b, H3)
                until(dve, "qq_ready", b, 2 * H3)
                until(dve, "qx_ready", b, H3)
                masked(0)
                masked(1)
                for m in range(NC * NEP):
                    if m + 2 < NC * NEP:
                        masked(m + 2)
                    until(dve, "mo_hi_ready", b, m + 1)
                    if m >= MO:
                        until(dve, "mo_used", b, m - MO + 1)
                    dve.tensor_tensor(mo_lo[:, m % MO, :], mo[:, m % MO, :], mo_hi[:, m % MO, :].bitcast(fp32),
                                      ALU.subtract).then_inc(sem["mo_lo_ready"], 1)
                    if 1 <= m <= TC:
                        normalise(PAIRS3 - 1, NC - 1, m - 1, TC)
                    if m == TC:
                        until(dve, "oT_ready", b, PAIRS3 * NC - 1 + TC)
                    if b + 1 < B and m % 6 == 4 and m // 6 < TT:
                        if m == 4:
                            dve.wait_ge(x_next, 16)
                        norm_stats(b + 1, 0, m // 6)
                    if b + 1 < B and m % 6 == 1 and 1 <= m // 6 <= TT:
                        norm_apply(b + 1, 0, m // 6 - 1)
                for i in range(TC):
                    if i % (TC // NC) == 0:
                        until(dve, "mo_used", b, NC * NEP - NC + 1 + i // (TC // NC))
                    dve.tensor_tensor(X[:, b, 2 * i:2 * i + 2, :],
                                      ps[:, 4 + i, :].rearrange("p (t n) -> p t n", t=2),
                                      X[:, b, 2 * i:2 * i + 2, :], ALU.add).then_inc(sem["out_ready"], 1)

        @block.tensor
        def _(pe):
            mm = pe.matmul

            def norm_transpose(b, a, t):
                idx = a * TT + t
                until(pe, "xn_ready", b, idx + 1)
                until(pe, "xT_ready", b, idx if b + a else idx - 1)
                for h in range(DA):
                    last = pe.transpose(ps[:, row_bank(b, a, t), h * P:(h + 1) * P],
                                        xn[:, t % 2, h * P:(h + 1) * P], ident)
                last.then_inc(sem["xnT_ps"], 1)

            def values(b, n):
                e, t = n // TT, n % TT
                g = b * PIECES + e
                if t == 0:
                    until(pe, "piece_lo", b, e + 1)
                if e == 0:
                    until(pe, "x_lo", b, t + 1)
                if 4 <= n < 4 + TT:
                    until(pe, "val_a", b, n - 3)
                elif n >= 4 + TT:
                    until(pe, "val_v", b, n - 3 - TT)
                rows_of, columns = slice(t * P, (t + 1) * P), lambda w, i: w[:, g % SLOTS, i * HK:(i + 1) * HK]
                parts = [(x, w, i) for i in range(DA)
                         for x, w in ((wide_hi, expert_hi), (wide_hi, expert_lo), (wide_lo, expert_hi))]
                for k, (x, w, i) in enumerate(parts):
                    last = mm(ps[:, n % 4, :], x[:, i, rows_of], columns(w, i),
                              start=(k == 0), stop=(k == len(parts) - 1))
                last.then_inc(sem["val_ps"], 1)

            def projection(n, bank, w, name):
                c, half = n // 2, n % 2
                for i in range(DA):
                    last = mm(ps[:, bank + n % 2, :], w[:, i, half * P:(half + 1) * P],
                              xT[:, i, c * CH:(c + 1) * CH], start=(i == 0), stop=(i == DA - 1))
                last.then_inc(sem[name], 1)

            def cross_keys_values():
                pe.wait_ge(kv_in, 16 * LOADS_KV)
                for a in range(DA):
                    for i in range(2):
                        last = mm(ps[:, a, 0:B * SKV], W2k[:, i, a * P:(a + 1) * P], ctxT[:, i, :],
                                  start=(i == 0), stop=(i == 1))
                last.then_inc(c2k_ps, 1)
                for bb in range(B):
                    for i in range(2):
                        last = mm(ps[0:SKV, 6 + bb, 0:D], ctxT[:, i, bb * SKV:(bb + 1) * SKV], W2v[:, i, :],
                                  start=(i == 0), stop=(i == 1))
                    last.then_inc(c2v_ps, 1)

            pe.wait_ge(const_in, 16)
            for t in range(TT):
                norm_transpose(0, 0, t)
            cross_keys_values()
            pe.wait_ge(front_in, 16 * LOADS_FRONT)
            for b in range(B):
                until(pe, "xT_ready", b, TT)
                for n in range(2 * NC):
                    if n >= 2:
                        until(pe, "k_sb", b, n - 1)
                    projection(n, 2, WkT, "k_ps")
                until(pe, "k_sb", b, 2 * NC)
                pe.wait_ge(c2k_sb, B)
                pe.wait_ge(c2v_sb, B)
                if b:
                    until(pe, "out_ready", b - 1, TC)
                for t in range(TT):
                    if t == 1:
                        until(pe, "kk_sb", b, 1)
                        for m in range(TT * DA):
                            last = mm(ps[:, 6, m * 8:m * 8 + 96], kk[:, m % DA, m // DA * P:(m // DA + 1) * P],
                                      head_of, start=(m == 0), stop=(m == TT * DA - 1), skip_group_check=True)
                        last.then_inc(sem["kk_ps"], 1)
                    if t >= 2:
                        until(pe, "fk_sub", b, t - 1)
                    for a in range(DA):
                        last = mm(ps[:, 2 - 2 * (t % 2) + a, :], kqT[:, a, t * P:(t + 1) * P], W0[:, a, :],
                                  start=True, stop=True)
                    last.then_inc(sem["fk_ps"], 1)
                    if t >= 2:
                        until(pe, "v_sb", b, t - 1)
                    for i in range(DA):
                        last = mm(ps[:, 4 + t % 2, 0:D], xT[:, i, t * P:(t + 1) * P], WvT[:, i, :],
                                  start=(i == 0), stop=(i == DA - 1))
                    last.then_inc(sem["v_ps"], 1)
                    for n in QUERIES_AT.get(t, ()):
                        until(pe, "q_sb", b, n)
                        projection(n, 7 - n % 2, WqT, "q_ps")
                until(pe, "fk_sub", b, TT - 1)
                if b == 0:
                    pe.wait_ge(later_in, 16 * LOADS_LATER)

                def gates(c):
                    until(pe, "xT_ready", b, 2 * TT + (c + 1) * TC)
                    until(pe, "cx_ready", b, 2 * TT)
                    if c:
                        until(pe, "var_ready", b, 3 * TT)
                    for t in range(TC):
                        for i in range(DA):
                            last = mm(ps[:, GATE_BANK[c], t * G:t * G + 96],
                                      xT[:, i, (c * TC + t) * P:(c * TC + t + 1) * P], Wg[:, i, :],
                                      start=(t + i == 0), stop=(t == TC - 1 and i == DA - 1), skip_group_check=True)
                    last.then_inc(sem["gate_ps"], 1)

                for s in range(LAST):
                    for a, t in due(s, 0):
                        if a == 0:
                            until(pe, "q_sb", b, 2 * (t // TC + 1))
                        else:
                            until(pe, "q2_sb", b, 2 * (t // TC + 1) if s <= TT + 5 else 2 * NC)
                            if t == 0:
                                pe.wait_ge(v2_placed, 16 * B * len(V2_RUNS))
                        until(pe, "f_sub", b, a * TT + t)
                        for i in range(DA):
                            if a == 0:
                                last = mm(ps[:, 2 + i, :], kqT[:, i, t * P:(t + 1) * P], W0[:, i, :],
                                          start=True, stop=True)
                            else:
                                last = mm(ps[:, 2 + i, 0:4 * SKV], kqT[:, i, t * P:(t + 1) * P],
                                          kblk[:, b, i, :], start=True, stop=True)
                        last.then_inc(sem["f_ps"], 1)
                    if s == 2:
                        until(pe, "n_blk", b, 2 * PAIRS1)
                        for k0, k1, w0 in N1_RUNS:
                            last = mm(ps[:, 6, 2 * k0:2 * k1], eps_blk,
                                      N1w[:, k0:k1, w0 + HD1:w0 + 2 * V1W:V1W], start=True, stop=True)
                        last.then_inc(sem["za_ps"], 1)
                    for a, t in due(s, 1):
                        until(pe, "f_exp", b, a * TT + t + 1)
                        until(pe, "fk_sub", b, TT)
                        until(pe, "fT_sb", b, a * TT + t)
                        for k in range((PAIRS1, K2C)[a]):
                            r = P if a == 0 else min(P, K2 - k * P)
                            last = pe.transpose(ps[0:r, k // TC, k % TC * P:(k % TC + 1) * P],
                                                phi[:, t % 2, k * P:k * P + r], ident)
                        last.then_inc(sem["fT_ps"], 1)
                    if s < 2:
                        until(pe, "e_ready", b, TT)
                        until(pe, "wv_ready", b, 1)
                        for p in range(s * PAIRS1 // 2, (s + 1) * PAIRS1 // 2):
                            for t in range(TT):
                                c0 = (t * PAIRS1 + p) * 2 * V1W
                                last = mm(ps[:, 4 + p // 4, p % 4 * P:p % 4 * P + WIN], E1[:, t, p * P:(p + 1) * P],
                                          V1_all[:, c0:c0 + WIN], start=(t == 0), stop=(t == TT - 1))
                        last.then_inc(sem["n_ps"], 1)
                    for a, t in due(s, 2):
                        until(pe, "fT_sb", b, a * TT + t + 1)
                        until(pe, "cx_ready", b, a * TT + t)
                        if a + t == 0:
                            until(pe, "n_ready", b, len(N1_RUNS))
                        chunks = (PAIRS1, K2C)[a]
                        for k in range(chunks):
                            if a == 0:
                                w0, w, r, src = N1_at(k), WIN, P, N1w[:, k, :]
                            else:
                                w0, w, r = FIRST2[k] * V2W, HEADS2[k] * V2W, min(P, K2 - k * P)
                                src = vblk[0:r, b, k, 0:w]
                            last = mm(ps[:, 6, w0:w0 + w], phT[0:r, t % 2, k * P:(k + 1) * P], src,
                                      start=(k == 0), stop=(k == chunks - 1), skip_group_check=True)
                        last.then_inc(sem["num_ps"], 1)
                    for a, t in due(s, 3):
                        until(pe, "cx_ready", b, a * TT + t + 1)
                        until(pe, "cxT_sb", b, a * TT + t)
                        for h in range(DA):
                            last = pe.transpose(ps[:, 4, h * P:(h + 1) * P], cx[:, t % 2, h * P:(h + 1) * P], ident)
                        last.then_inc(sem["cxT_ps"], 1)
                    for a, t in due(s, 4):
                        until(pe, "cxT_sb", b, a * TT + t + 1)
                        if a + t:
                            until(pe, "var_ready", b, (a + 1) * TT + t)
                        for i in range(DA):
                            last = mm(ps[:, 5, 0:D], cxT[:, t % 2, i, :], (WoT, W2o)[a][:, i, :],
                                      start=(i == 0), stop=(i == DA - 1))
                        last.then_inc(sem["y_ps"], 1)
                    for a, t in due(s, 6):
                        norm_transpose(b, a + 1, t)
                        if a == 0 and t % TC == TC - 1:
                            until(pe, "xT_ready", b, TT + t + 1)
                            until(pe, "f_sub", b, TT + max(0, s - OFFSET[1] + 1))
                            for n in range(2 * (t // TC), 2 * (t // TC) + 2):
                                if n >= 2:
                                    until(pe, "q2_sb", b, n - 1)
                                projection(n, 2, W2q, "q2_ps")
                    if s in GATES_AT:
                        gates(GATES_AT.index(s))
                    if 0 <= (t := s - VALUES_AT) < TT:
                        until(pe, "xT_ready", b, 2 * TT + t + 1)
                        if t == 0:
                            until(pe, "f_sub", b, 2 * TT)
                            until(pe, "fT_sb", b, 2 * TT)
                        values(b, t)

                def project(p, n):
                    which, c = n // NC, n % NC
                    until(pe, "qk_sb", b, p * 2 * NC + n)
                    if n in (0, 2 * NC - 1) and p:
                        until(pe, "m_row", b, 2 * p - 1 + (n > 0))
                    parts = [(w, x, i) for i in range(DA)
                             for w, x in ((W3_hi, wide_hi), (W3_lo, wide_hi), (W3_hi, wide_lo))]
                    for k, (w, x, i) in enumerate(parts):
                        last = mm(ps[:, 6, :], w[:, which, i, p * P:(p + 1) * P], x[:, i, c * CH:(c + 1) * CH],
                                  start=(k == 0), stop=(k == len(parts) - 1))
                    last.then_inc(sem["qk_ps"], 1)

                def scores(h, m):
                    i, (t, c) = h % 2, SCORES[m]
                    if h == 0 and m == 0:
                        until(pe, "gT_v", b, 1)
                    if h == 1 and m == 0:
                        until(pe, "val_v", b, TT * (E3 - 1))
                    if m == 0:
                        until(pe, "qq_ready", b, 2 * h + 2)
                        until(pe, "kst_ready", b, 2 * h + 2)
                    until(pe, "s_max", b, h * NB + m + 1 - MAX_BANKS)
                    w, diagonal = min(CH, (t + 1) * P - c * CH), c == t // TC
                    last = mm(ps[:, max_bank(h, m), 0:w], qq[i][:, t * P:(t + 1) * P], kst[i][:, c * CH:c * CH + w],
                              start=True, stop=not diagonal)
                    if diagonal:
                        last = mm(ps[:, max_bank(h, m), w - P:w], ident_b[:, :], neg[:, 0, :], start=False, stop=True)
                    last.then_inc(sem["s_ps"], 1)

                def max_rows(h):
                    until(pe, "tile_max", b, h + 1)
                    until(pe, "qk_sb", b, min((h + 1) // 2 + 1, PAIRS3) * 2 * NC - (h % 2 and h + 1 < H3))
                    pe.transpose(ps[0:TT, 6, 0:P], mx[:, h % 2, 0:TT], ident).then_inc(sem["mxT_ps"], 1)

                def weigh(g):
                    h, (c, j) = g // NB, BLOCKS[g % NB]
                    lo = max(0, j - TC * c) * P
                    until(pe, "pt_ready", b, g + 1)
                    if h == 0 and j >= TC * c:
                        until(pe, "v3_ready", b, j + 2)
                    if g == 0:
                        until(pe, "val_v", b, TT * (E3 - 1))
                    if j == 0 and h:
                        until(pe, "o_sb", b, 2 * ((h - 1) * NC + c + 1))
                    mm(ps[:, SUM_BANK[c], lo:CH], V3[:, j, h // 2, h % 2 * HD3:(h % 2 + 2) * HD3],
                       PT[:, g % RING, lo:CH], start=(j == 0), stop=(j == TC * (c + 1) - 1)
                       ).then_inc(sem["av_used"], 1)

                if b == 0:
                    pe.wait_ge(w3_lo, 2)
                    pe.wait_ge(casts, 2)
                    pe.wait_ge(cleared, SETUP)
                for n in range(TT, TT * E3):
                    if n == TT + 1:
                        until(pe, "g_ready", b, NC)
                        for k in range(TT):
                            last = pe.transpose(ps[0:G, 4 + k // TC, k % TC * P:(k % TC + 1) * P],
                                                gw[:, k, :, :].rearrange("p h e -> p (h e)"), ident)
                        last.then_inc(sem["gT_ps"], 1)
                    values(b, n)
                    if n in range(PROJECT_FIRST, PROJECT_FIRST + TT, 2):
                        project(0, (n - PROJECT_FIRST) // 2)
                    if 0 <= n - SCORES_FIRST < NB:
                        scores(0, n - SCORES_FIRST)
                    if n == SCORES_FIRST + NB + 1:
                        max_rows(0)
                def mask(m):
                    n, c = m // NC, m % NC
                    e, p = n // PAIRS3, n % PAIRS3
                    until(pe, "mo_ready", b, m - AHEAD + 1)
                    until(pe, "picks_ready", b, e + 1)
                    mm(ps[:, m % AHEAD, :], picks(e)[:, p * P:(p + 1) * P], gT[:, c * CH:(c + 1) * CH],
                       start=True, stop=True).then_inc(sem["mask_ps"], 1)

                for h in range(H3):
                    i = h % 2
                    if h == H3 - 1:
                        until(pe, "s_max", b, H3 * NB)
                    until(pe, "kx_ready", b, h + 1)
                    until(pe, "qx_ready", b, h + 1)
                    until(pe, "m_row", b, h + 1)
                    for n, (c, j) in enumerate(BLOCKS):
                        lo, g = max(0, j - TC * c) * P, h * NB + n
                        w = CH - lo
                        until(pe, "pt_ready", b, g - 1)
                        bank, key, query = 4 + g % 2, slice(j * P, (j + 1) * P), slice(c * CH + lo, (c + 1) * CH)
                        mm(ps[:, bank, 0:w], kst[i][:, key], qq[i][:, query], start=True, stop=False)
                        last = mm(ps[:, bank, 0:w], kx[i][:, key], qx[i][:, query], start=False, stop=j < TC * c)
                        if j >= TC * c:
                            last = mm(ps[:, bank, 0:P], ident_b[:, :], neg[:, 1, :], start=False, stop=True)
                        last.then_inc(sem["st_ps"], 1)
                        if g >= LAG:
                            weigh(g - LAG)
                        if n in PROJECT_AT and h % 2 == 0 and h + 2 < H3:
                            project(h // 2 + 1, PROJECT_AT.index(n))
                        if h + 1 == H3 and n == MASKS_AT:
                            for m in range(AHEAD):
                                mask(m)
                        if h + 1 < H3:
                            for m in SCORES_AT.get(n, ()):
                                scores(h + 1, m)
                            if n == MAX_ROW_AT:
                                max_rows(h + 1)
                for g in range(H3 * NB - LAG, H3 * NB):
                    weigh(g)
                until(pe, "pt_ready", b, H3 * NB)
                for m in range(NC * NEP):
                    n, c = m // NC, m % NC
                    e, p = n // PAIRS3, n % PAIRS3
                    g = b * PIECES + E3 + e
                    if m + AHEAD < NC * NEP:
                        mask(m + AHEAD)
                    if p == 0 and c == 0:
                        until(pe, "piece_lo", b, E3 + e + 1)
                    if m == 1:
                        until(pe, "o_sb", b, 2 * H3 * NC)
                    until(pe, "mo_lo_ready", b, m + 1)
                    for k in range(TC):
                        t = c * TC + k
                        for r, w in ((mo_hi, expert_hi), (mo_hi, expert_lo), (mo_lo, expert_hi)):
                            last = mm(ps[:, 4 + t // 2, t % 2 * D:(t % 2 + 1) * D], r[:, m % MO, k * P:(k + 1) * P],
                                      w[:, g % SLOTS, p * D:(p + 1) * D],
                                      start=(n == 0 and t % 2 == 0 and r is mo_hi and w is expert_hi),
                                      stop=(n == NEP - 1 and r is mo_lo), skip_group_check=True)
                    last.then_inc(sem["mo_used"], 1)
                    if b + 1 < B and m % 6 == 3 and 1 <= m // 6 <= TT:
                        norm_transpose(b + 1, 0, m // 6 - 1)


def kernel(x, ctx_768, L0_attn_Wq, L0_attn_bq, L0_attn_Wk, L0_attn_bk, L0_attn_Wv, L0_attn_bv, L0_attn_Wo,
           L0_attn_bo, L0_attn_Wrf, L0_xattn_Wq, L0_xattn_bq, L0_xattn_Wk, L0_xattn_bk, L0_xattn_Wv,
           L0_xattn_bv, L0_xattn_Wo, L0_xattn_bo, L0_ffn_w_q, L0_ffn_w_k, L0_ffn_w_gate,
           L0_ffn_value_experts, L0_ffn_output_experts):
    import numpy as np
    import concourse.bacc as bacc
    from concourse.bass_utils import run_bass_kernel_spmd

    P = 128
    arr = lambda a: np.asarray(a)

    def halves(w):
        w = arr(w)
        return w.reshape(w.shape[0] // P, P, -1).transpose(1, 0, 2)

    x, c = arr(x), arr(ctx_768)
    B, S, D = x.shape
    DC = c.shape[2]
    f = x.dtype
    wrf = arr(L0_attn_Wrf)[0]
    H1, HD1, NF = wrf.shape
    w0 = np.zeros((2, 8, HD1, 8, NF), f)
    for h in range(H1):
        w0[h // 8, h % 8, :, h % 8, :] = wrf[h]
    ve, oe = arr(L0_ffn_value_experts), arr(L0_ffn_output_experts)
    E, H, _, K = ve.shape
    ve = ve.reshape(E, H, 2, P, K).transpose(3, 0, 2, 1, 4).reshape(P, E, 2 * H * K)
    oe = oe.reshape(E, H // 2, 2, K, D).transpose(2, 3, 0, 1, 4).reshape(P, E, H // 2 * D)
    two = lambda v: arr(v).reshape(2, P).T
    r, k = np.arange(P)[:, None], np.arange(P)[None, :]
    tri = np.where(k > r, -1e30, 0.0)
    TT = S // P
    const = np.concatenate([
        np.eye(P), np.where(r // NF == k // NF, 1e-6, 0.0),
        (r // HD1 == np.arange(96)[None, :]), (r % (H * E) == np.arange(H * E)[None, :]),
        np.tile(np.arange(E)[None, :], (P, 1))], axis=1).astype(f)
    data = {
        "x": x,
        "ctxT": c.reshape(B * c.shape[1], 2, DC // 2).transpose(2, 1, 0),
        "WkT": halves(arr(L0_attn_Wk).T), "WqT": halves(arr(L0_attn_Wq).T),
        "WvT": halves(arr(L0_attn_Wv).T), "WoT": halves(arr(L0_attn_Wo).T),
        "W0": w0.reshape(2, P, 8 * NF).transpose(1, 0, 2),
        "W2q": halves(L0_xattn_Wq), "W2o": halves(L0_xattn_Wo),
        "W2k": arr(L0_xattn_Wk).reshape(2, DC // 2, D).transpose(1, 0, 2),
        "W2v": arr(L0_xattn_Wv).reshape(2, DC // 2, D).transpose(1, 0, 2),
        "Wg": np.concatenate([halves(L0_ffn_w_gate), np.zeros((P, 2, 96 - E * H), f)], axis=2),
        "W3q": halves(L0_ffn_w_q).reshape(P, -1), "W3k": halves(L0_ffn_w_k).reshape(P, -1),
        "value_experts": ve, "output_experts": oe,
        "cols": np.concatenate([two(L0_attn_bq), two(L0_attn_bk), two(L0_xattn_bq), two(L0_xattn_bk)], axis=1),
        "rows": np.broadcast_to(np.stack([arr(L0_attn_bv), arr(L0_attn_bo), arr(L0_xattn_bo)])[None], (P, 3, D)),
        "bv2": np.broadcast_to(arr(L0_xattn_bv)[None], (P, D)),
        "neg_f": np.stack([tri, tri.T], axis=1).astype(f),
        "const": const,
    }
    nc = bacc.Bacc("TRN2", target_bir_lowering=False, num_devices=1)
    arrays, d = {}, {}
    from concourse import mybir
    for name, a in data.items():
        a = np.ascontiguousarray(a)
        arrays[f"in_{name}"] = a
        d[name] = nc.dram_tensor(f"in_{name}", a.shape, mybir.dt.from_np(a.dtype), kind="ExternalInput").ap()
    out = nc.dram_tensor("out_0", (B, S, D), mybir.dt.from_np(x.dtype), kind="ExternalOutput").ap()
    decoder_layer(nc, d, out)
    got = run_bass_kernel_spmd(nc, [arrays], core_ids=[0])
    return got.results[0]["out_0"]
```
